# Optimizing a Trainium2 kernel written in Bass

```python
import numpy as np
import jax
import jax.numpy as jnp

def _softmax(x, axis=-1):
    return jax.nn.softmax(x, axis=axis)

def _gelu(x):
    return jax.nn.gelu(x, approximate=True)

def _silu(x):
    return jax.nn.silu(x)

def _sigmoid(x):
    return jax.nn.sigmoid(x)

def _layernorm(x, axis=-1, eps=1e-05):
    m = jnp.mean(x, axis=axis, keepdims=True)
    v = jnp.var(x, axis=axis, keepdims=True)
    return (x - m) / jnp.sqrt(v + eps)

def _scatter_add(tgt, idx, src, axis=0):
    return tgt.at[idx].add(src)

def _segment_sum(src, seg, n):
    return jax.ops.segment_sum(src, seg, n)
kernel_name = 'mk_perceiver_d1_seqx_r8_3adc09'

def setup_inputs(seed: int=0):
    np.random.seed(seed)
    _w = jnp.asarray

    def _rec_inputs():
        import jax
        import jax.numpy as jnp
        _rk = jax.random.key(seed)
        x = -0.0002928 + 1 * jax.random.normal(jax.random.fold_in(_rk, 1), (128, 32, 128), jnp.float32)
        _lenS = 32 - jax.random.randint(jax.random.fold_in(_rk, 7), (128,), 0, max(1, 32 // 4) + 1, jnp.int32)
        _lenS2 = 257 - jax.random.randint(jax.random.fold_in(_rk, 8), (128,), 0, max(1, 257 // 4) + 1, jnp.int32)
        _ctx_1024P = jax.random.normal(jax.random.fold_in(_rk, 11), (128, 16, 128), jnp.float32)
        _ctx_1024c = jax.random.dirichlet(jax.random.fold_in(_rk, 511), 0.3 * jnp.ones((16,), jnp.float32), (128, 257))
        _ctx_1024t = jnp.einsum('bsk,bkd->bsd', _ctx_1024c, _ctx_1024P)
        _ctx_1024t = _ctx_1024t * jax.lax.rsqrt(jnp.mean(jnp.square(_ctx_1024t)) + 1e-12) * 0.953939
        ctx_1024 = -1.39393e-06 + 0.999914 * (_ctx_1024t + 0.3 * jax.random.normal(jax.random.fold_in(_rk, 611), (128, 257, 128), jnp.float32))
        _validS = jnp.arange(32)[None, :] < _lenS[:, None]
        _validS2 = jnp.arange(257)[None, :] < _lenS2[:, None]
        _causal = jnp.tril(jnp.ones((32, 32), dtype=bool))
        mask_Bx1xSxS2_bf0 = jnp.logical_not(jnp.ones((128, 1, 32, 257), dtype=bool))
        return (x, ctx_1024, mask_Bx1xSxS2_bf0)
    x, ctx_1024, mask_Bx1xSxS2_bf0 = _rec_inputs()

    def _L0_xattn_setup():
        import jax, jax.numpy as jnp
        import numpy as np
        B, S, D, H = (2, 256, 128, 16)
        HD = D // H
        LN_EPS = 1e-05

        def _linear(x, w, b):
            return jnp.einsum('bsd,od->bso', x, w) + b

        def _split_heads(x):
            b, s, _ = x.shape
            return x.reshape(b, s, H, HD).transpose(0, 2, 1, 3)
        key = jax.random.key(seed)
        ks = jax.random.split(key, 14)
        w = 0.02
        return {'q': jax.random.normal(ks[0], (B, S, D), jnp.float32), 'k': jax.random.normal(ks[1], (B, S, D), jnp.float32), 'v': jax.random.normal(ks[2], (B, S, D), jnp.float32), 'mask': jnp.zeros((B, 1, S, S), dtype=bool), 'training': 0, 'wq_w': jax.random.normal(ks[3], (D, D), jnp.float32) * w, 'wq_b': jnp.zeros((D,), jnp.float32), 'wk_w': jax.random.normal(ks[4], (D, D), jnp.float32) * w, 'wk_b': jnp.zeros((D,), jnp.float32), 'wv_w': jax.random.normal(ks[5], (D, D), jnp.float32) * w, 'wv_b': jnp.zeros((D,), jnp.float32), 'wo_w': jax.random.normal(ks[6], (D, D), jnp.float32) * w, 'wo_b': jnp.zeros((D,), jnp.float32), 'ln_g': jnp.ones((D,), jnp.float32), 'ln_b': jnp.zeros((D,), jnp.float32)}
    _L0_xattn_all = _L0_xattn_setup()
    _L0_xattn_in = {k: v for k, v in _L0_xattn_all.items() if k in ('wq_w', 'wq_b', 'wk_w', 'wk_b', 'wv_w', 'wv_b', 'wo_w', 'wo_b', 'ln_g', 'ln_b')}
    del _L0_xattn_all

    def _L0_attn_setup():
        import jax, jax.numpy as jnp
        import numpy as np
        import math
        D_MODEL = 128
        NUM_HEADS = 16
        D_HEAD = D_MODEL // NUM_HEADS
        B, T = (8, 128)

        def rel_pos_encoding(seq_len, d, dtype=jnp.float32):
            pos = jnp.arange(seq_len, dtype=jnp.float32)[:, None]
            div = jnp.exp(jnp.arange(0, d, 2, dtype=jnp.float32) * (-math.log(10000.0) / d))
            ang = pos * div
            pe_pos = jnp.stack([jnp.sin(ang), jnp.cos(ang)], axis=-1).reshape(seq_len, d)
            pe_neg = jnp.stack([jnp.sin(-ang), jnp.cos(-ang)], axis=-1).reshape(seq_len, d)
            pe = jnp.concatenate([pe_pos[::-1], pe_neg[1:]], axis=0)
            return pe.astype(dtype)

        def _rel_shift(pos_score):
            b, h, t1, t2 = pos_score.shape
            padded = jnp.pad(pos_score, ((0, 0), (0, 0), (0, 0), (1, 0)))
            padded = padded.reshape(b, h, t2 + 1, t1)
            return padded[:, :, 1:].reshape(b, h, t1, t2)[:, :, :, :t1]
        key = jax.random.key(seed)
        ks = jax.random.split(key, 9)
        D = D_MODEL
        s = 1.0 / math.sqrt(D)
        return {'x': jax.random.normal(ks[0], (B, T, D), jnp.float32), 'Wq': jax.random.normal(ks[1], (D, D), jnp.float32) * s, 'bq': jnp.zeros((D,), jnp.float32), 'Wk': jax.random.normal(ks[2], (D, D), jnp.float32) * s, 'bk': jnp.zeros((D,), jnp.float32), 'Wv': jax.random.normal(ks[3], (D, D), jnp.float32) * s, 'bv': jnp.zeros((D,), jnp.float32), 'Wpos': jax.random.normal(ks[4], (D, D), jnp.float32) * s, 'Wout': jax.random.normal(ks[5], (D, D), jnp.float32) * s, 'bout': jnp.zeros((D,), jnp.float32), 'u_bias': jax.random.normal(ks[6], (NUM_HEADS, D_HEAD), jnp.float32) * 0.1, 'v_bias': jax.random.normal(ks[7], (NUM_HEADS, D_HEAD), jnp.float32) * 0.1, 'ln_gamma': jnp.ones((D,), jnp.float32), 'ln_beta': jnp.zeros((D,), jnp.float32)}
    _L0_attn_all = _L0_attn_setup()
    _L0_attn_in = {k: v for k, v in _L0_attn_all.items() if k in ('Wq', 'bq', 'Wk', 'bk', 'Wv', 'bv', 'Wpos', 'Wout', 'bout', 'u_bias', 'v_bias', 'ln_gamma', 'ln_beta')}
    del _L0_attn_all

    def _L0_ffn_setup():
        import jax, jax.numpy as jnp
        import numpy as np
        BEST_K = 2

        def _expert(xf, w1, w3, w2):
            return jax.nn.silu(xf @ w1) * (xf @ w3) @ w2
        key = jax.random.key(seed)
        ks = jax.random.split(key, 9)
        E, S_sh, D, H = (8, 2, 128, 64)
        B, S = (2, 256)
        w = lambda k, shape: jax.random.normal(k, shape, dtype=jnp.float32) * 0.02
        return {'x': jax.random.normal(ks[0], (B, S, D), dtype=jnp.float32), 'router_w': w(ks[1], (D, E)), 'router_b': jnp.zeros((E,), dtype=jnp.float32), 'routed_w1': w(ks[2], (E, D, H)), 'routed_w3': w(ks[3], (E, D, H)), 'routed_w2': w(ks[4], (E, H, D)), 'shared_w1': w(ks[5], (S_sh, D, H)), 'shared_w3': w(ks[6], (S_sh, D, H)), 'shared_w2': w(ks[7], (S_sh, H, D))}
    _L0_ffn_all = _L0_ffn_setup()
    _L0_ffn_in = {k: v for k, v in _L0_ffn_all.items() if k in ('router_w', 'router_b', 'routed_w1', 'routed_w3', 'routed_w2', 'shared_w1', 'shared_w3', 'shared_w2')}
    del _L0_ffn_all
    return {'x': x, 'ctx_1024': ctx_1024, 'mask_Bx1xSxS2_bf0': mask_Bx1xSxS2_bf0, 'L0_xattn_wq_w': _L0_xattn_in['wq_w'], 'L0_xattn_wq_b': _L0_xattn_in['wq_b'], 'L0_xattn_wk_w': _L0_xattn_in['wk_w'], 'L0_xattn_wk_b': _L0_xattn_in['wk_b'], 'L0_xattn_wv_w': _L0_xattn_in['wv_w'], 'L0_xattn_wv_b': _L0_xattn_in['wv_b'], 'L0_xattn_wo_w': _L0_xattn_in['wo_w'], 'L0_xattn_wo_b': _L0_xattn_in['wo_b'], 'L0_xattn_ln_g': _L0_xattn_in['ln_g'], 'L0_xattn_ln_b': _L0_xattn_in['ln_b'], 'L0_attn_Wq': _L0_attn_in['Wq'], 'L0_attn_bq': _L0_attn_in['bq'], 'L0_attn_Wk': _L0_attn_in['Wk'], 'L0_attn_bk': _L0_attn_in['bk'], 'L0_attn_Wv': _L0_attn_in['Wv'], 'L0_attn_bv': _L0_attn_in['bv'], 'L0_attn_Wpos': _L0_attn_in['Wpos'], 'L0_attn_Wout': _L0_attn_in['Wout'], 'L0_attn_bout': _L0_attn_in['bout'], 'L0_attn_u_bias': _L0_attn_in['u_bias'], 'L0_attn_v_bias': _L0_attn_in['v_bias'], 'L0_attn_ln_gamma': _L0_attn_in['ln_gamma'], 'L0_attn_ln_beta': _L0_attn_in['ln_beta'], 'L0_ffn_router_w': _L0_ffn_in['router_w'], 'L0_ffn_router_b': _L0_ffn_in['router_b'], 'L0_ffn_routed_w1': _L0_ffn_in['routed_w1'], 'L0_ffn_routed_w3': _L0_ffn_in['routed_w3'], 'L0_ffn_routed_w2': _L0_ffn_in['routed_w2'], 'L0_ffn_shared_w1': _L0_ffn_in['shared_w1'], 'L0_ffn_shared_w3': _L0_ffn_in['shared_w3'], 'L0_ffn_shared_w2': _L0_ffn_in['shared_w2']}

def reference(x, ctx_1024, mask_Bx1xSxS2_bf0, L0_xattn_wq_w, L0_xattn_wq_b, L0_xattn_wk_w, L0_xattn_wk_b, L0_xattn_wv_w, L0_xattn_wv_b, L0_xattn_wo_w, L0_xattn_wo_b, L0_xattn_ln_g, L0_xattn_ln_b, L0_attn_Wq, L0_attn_bq, L0_attn_Wk, L0_attn_bk, L0_attn_Wv, L0_attn_bv, L0_attn_Wpos, L0_attn_Wout, L0_attn_bout, L0_attn_u_bias, L0_attn_v_bias, L0_attn_ln_gamma, L0_attn_ln_beta, L0_ffn_router_w, L0_ffn_router_b, L0_ffn_routed_w1, L0_ffn_routed_w3, L0_ffn_routed_w2, L0_ffn_shared_w1, L0_ffn_shared_w3, L0_ffn_shared_w2):
    import jax
    import jax.numpy as jnp

    def _L0_xattn_ref(q, k, v, mask, training, wq_w, wq_b, wk_w, wk_b, wv_w, wv_b, wo_w, wo_b, ln_g, ln_b):
        import jax, jax.numpy as jnp
        import numpy as np
        B, S, D, H = (2, 256, 128, 16)
        HD = D // H
        LN_EPS = 1e-05

        def _linear(x, w, b):
            return jnp.einsum('bsd,od->bso', x, w) + b

        def _split_heads(x):
            b, s, _ = x.shape
            return x.reshape(b, s, H, HD).transpose(0, 2, 1, 3)
        residual = q
        Q = _split_heads(_linear(q, wq_w, wq_b))
        K = _split_heads(_linear(k, wk_w, wk_b))
        V = _split_heads(_linear(v, wv_w, wv_b))
        dk = jnp.sqrt(jnp.asarray(HD, jnp.float16)).astype(jnp.float32) + 1e-08
        score = jnp.einsum('bhqd,bhkd->bhqk', Q, K) / dk
        attn = jnp.where(mask, -jnp.inf, score)
        ctx = jnp.einsum('bhqk,bhkd->bhqd', attn, V)
        b, _, s, _ = ctx.shape
        ctx = ctx.transpose(0, 2, 1, 3).reshape(b, s, D)
        o = _linear(ctx, wo_w, wo_b)
        x = residual + o
        mu = jnp.mean(x, axis=-1, keepdims=True)
        var = jnp.mean(jnp.square(x - mu), axis=-1, keepdims=True)
        return ln_g * (x - mu) * jax.lax.rsqrt(var + LN_EPS) + ln_b

    def _L0_attn_ref(x, Wq, bq, Wk, bk, Wv, bv, Wpos, Wout, bout, u_bias, v_bias, ln_gamma, ln_beta):
        import jax, jax.numpy as jnp
        import numpy as np
        import math
        D_MODEL = 128
        NUM_HEADS = 16
        D_HEAD = D_MODEL // NUM_HEADS
        B, T = (8, 128)

        def rel_pos_encoding(seq_len, d, dtype=jnp.float32):
            pos = jnp.arange(seq_len, dtype=jnp.float32)[:, None]
            div = jnp.exp(jnp.arange(0, d, 2, dtype=jnp.float32) * (-math.log(10000.0) / d))
            ang = pos * div
            pe_pos = jnp.stack([jnp.sin(ang), jnp.cos(ang)], axis=-1).reshape(seq_len, d)
            pe_neg = jnp.stack([jnp.sin(-ang), jnp.cos(-ang)], axis=-1).reshape(seq_len, d)
            pe = jnp.concatenate([pe_pos[::-1], pe_neg[1:]], axis=0)
            return pe.astype(dtype)

        def _rel_shift(pos_score):
            b, h, t1, t2 = pos_score.shape
            padded = jnp.pad(pos_score, ((0, 0), (0, 0), (0, 0), (1, 0)))
            padded = padded.reshape(b, h, t2 + 1, t1)
            return padded[:, :, 1:].reshape(b, h, t1, t2)[:, :, :, :t1]
        b, t, d = x.shape
        h, dh = (NUM_HEADS, D_HEAD)
        mu = jnp.mean(x, axis=-1, keepdims=True)
        var = jnp.mean((x - mu) ** 2, axis=-1, keepdims=True)
        xn = (x - mu) * jax.lax.rsqrt(var + 1e-05) * ln_gamma + ln_beta
        pos_emb = rel_pos_encoding(t, d, x.dtype)
        q = (xn @ Wq.T + bq).reshape(b, t, h, dh)
        k = (xn @ Wk.T + bk).reshape(b, t, h, dh)
        v = (xn @ Wv.T + bv).reshape(b, t, h, dh)
        p = (pos_emb @ Wpos.T).reshape(2 * t - 1, h, dh)
        content_score = jnp.einsum('bthd,bshd->bhts', q + u_bias, k)
        pos_score = jnp.einsum('bthd,phd->bhtp', q + v_bias, p)
        pos_score = _rel_shift(pos_score)
        score = (content_score + pos_score) / math.sqrt(dh)
        attn = jax.nn.softmax(score, axis=-1)
        ctx = jnp.einsum('bhts,bshd->bthd', attn, v).reshape(b, t, d)
        return ctx @ Wout.T + bout

    def _L0_ffn_ref(x, router_w, router_b, routed_w1, routed_w3, routed_w2, shared_w1, shared_w3, shared_w2):
        import jax, jax.numpy as jnp
        import numpy as np
        BEST_K = 2

        def _expert(xf, w1, w3, w2):
            return jax.nn.silu(xf @ w1) * (xf @ w3) @ w2
        B, S, D = x.shape
        T = B * S
        xf = x.reshape(T, D)
        logits = xf @ router_w + router_b
        topk_vals, topk_idx = jax.lax.top_k(logits, BEST_K)
        sparse = jnp.full_like(logits, -jnp.inf)
        sparse = sparse.at[jnp.arange(T)[:, None], topk_idx].set(topk_vals)
        gates = jax.nn.softmax(sparse, axis=-1)
        routed = jax.vmap(_expert, in_axes=(None, 0, 0, 0))(xf, routed_w1, routed_w3, routed_w2)
        routed_out = jnp.einsum('etd,te->td', routed, gates)
        shared_out = jax.vmap(_expert, in_axes=(None, 0, 0, 0))(xf, shared_w1, shared_w3, shared_w2).sum(axis=0)
        return (routed_out + shared_out).reshape(B, S, D)
    x = x + _L0_xattn_ref(_layernorm(x, axis=-1), ctx_1024, ctx_1024, mask_Bx1xSxS2_bf0, 0, L0_xattn_wq_w, L0_xattn_wq_b, L0_xattn_wk_w, L0_xattn_wk_b, L0_xattn_wv_w, L0_xattn_wv_b, L0_xattn_wo_w, L0_xattn_wo_b, L0_xattn_ln_g, L0_xattn_ln_b)
    x = x + _L0_attn_ref(_layernorm(x, axis=-1), L0_attn_Wq, L0_attn_bq, L0_attn_Wk, L0_attn_bk, L0_attn_Wv, L0_attn_bv, L0_attn_Wpos, L0_attn_Wout, L0_attn_bout, L0_attn_u_bias, L0_attn_v_bias, L0_attn_ln_gamma, L0_attn_ln_beta)
    x = x + _L0_ffn_ref(_layernorm(x, axis=-1), L0_ffn_router_w, L0_ffn_router_b, L0_ffn_routed_w1, L0_ffn_routed_w3, L0_ffn_routed_w2, L0_ffn_shared_w1, L0_ffn_shared_w3, L0_ffn_shared_w2)
    return x

_drawn_inputs = setup_inputs


def setup_inputs(seed=0):
    import zlib

    import numpy as np

    out = dict(_drawn_inputs(seed))
    spreads = {'L0_xattn_wq_b': (0.0, 0.1),
     'L0_xattn_wk_b': (0.0, 0.1),
     'L0_xattn_wv_b': (0.0, 0.1),
     'L0_xattn_wo_b': (0.0, 0.1),
     'L0_xattn_ln_g': (1.0, 0.2),
     'L0_xattn_ln_b': (0.0, 0.1),
     'L0_attn_bq': (0.0, 0.629),
     'L0_attn_bk': (0.0, 0.8),
     'L0_attn_bv': (0.0, 0.1),
     'L0_attn_bout': (0.0, 0.1),
     'L0_attn_ln_gamma': (1.0, 0.2),
     'L0_attn_ln_beta': (0.0, 0.1),
     'L0_ffn_router_b': (0.0, 0.8)}
    factors = {'L0_attn_u_bias': 3.789,
     'L0_attn_v_bias': 8.0,
     'L0_ffn_router_w': 8.0,
     'L0_ffn_routed_w1': 8.0,
     'L0_ffn_routed_w3': 8.0,
     'L0_ffn_routed_w2': 8.0,
     'L0_ffn_shared_w1': 8.0,
     'L0_ffn_shared_w3': 8.0,
     'L0_ffn_shared_w2': 8.0}
    for name, (base, spread) in spreads.items():
        noise = np.random.default_rng([zlib.crc32(name.encode()), seed]).standard_normal(out[name].shape)
        drawn = base * np.exp(spread * noise) if base else spread * noise
        out[name] = jnp.asarray(drawn.astype(out[name].dtype))
    for name, factor in factors.items():
        out[name] = (out[name] * factor).astype(out[name].dtype)
    return out
```

```python
import math

import numpy as np

import concourse.bass as bass
from concourse import mybir

NB, S, D = 128, 32, 128
S2 = 257
HEADS, HD = 16, 8
P = 128
BT = P // S
TILES = NB // BT
HG = P // S
POS = 2 * S - 1
EXPERTS, HID, SHARED = 8, 64, 2
FR, FS = EXPERTS * HID, SHARED * HID
FF = FR + FS
CHUNKS = FF // P
EPS = 1e-5
DK = float(np.float32(np.sqrt(np.float16(HD))) + np.float32(1e-8))
GW = D + 1
OW = 36

WEIGHT_BLOCKS = [
    ("xwq", D), ("xwk", D), ("xwv", D), ("xwo", D),
    ("awq", D), ("awk", D), ("awv", D), ("awp", D), ("awo", D),
    ("w1", FF), ("w3", FF), ("w2", FF), ("router", EXPERTS),
    ("xbq", 1), ("xbk", 1), ("xbv", 1), ("abq", 1), ("abk", 1), ("u", 1), ("v", 1), ("gamma", 1), ("beta", 1),
    ("pe", POS), ("ident", P), ("blk32", 32), ("blk128", P), ("head16", HEADS), ("vmask", 32), ("ones4", 4),
    ("batch_row", P), ("batch_tile", TILES), ("lower", EXPERTS * EXPERTS),
]
ROW_BLOCKS = [("xbv", D), ("xbo", D), ("ln_g", D), ("ln_b", D), ("abv", D), ("abo", D), ("rb", EXPERTS)]


def offsets(blocks):
    at, out = 0, {}
    for name, n in blocks:
        out[name] = (at, n)
        at += n
    return out, at


WEIGHT_AT, WEIGHT_COLS = offsets(WEIGHT_BLOCKS)
ROW_AT, ROW_COLS = offsets(ROW_BLOCKS)


def perceiver_kernel(nc, x, ctx_main, ctx_last, mask, weights, rows, out, pos_scratch, v_scratch):
    f32 = mybir.dt.float32
    ALU = mybir.AluOpType
    ACT = mybir.ActivationFunctionType
    AX = mybir.AxisListType.X

    from contextlib import ExitStack

    ctx = ExitStack()
    with ctx:
        def sb(name, shape, dt=f32):
            return ctx.enter_context(nc.sbuf_tensor(name, shape, dt))

        def sem(name):
            return ctx.enter_context(nc.semaphore(name))

        w_sb = sb("w_sb", [P, WEIGHT_COLS])
        row_sb = sb("row_sb", [P, ROW_COLS])

        def W(name):
            at, n = WEIGHT_AT[name]
            return w_sb[:, at:at + n]

        def ROW(name):
            at, n = ROW_AT[name]
            return row_sb[:, at:at + n]

        x_all = sb("x_all", [P, TILES, D])
        q_all = sb("q_all", [P, NB, S])
        k_all = sb("k_all", [P, NB * S])
        half = sb("half", [P, 1])
        poison = sb("poison", [P, TILES])
        cols = sb("cols", [P, 8])
        xbq_s, xbv_n, qu_b, qv_b = (cols[:, n:n + 1] for n in range(4))
        bk_heads = sb("bk_heads", [P, P])
        pos_blk = sb("pos_blk", [P, HEADS, POS])
        mask_sb = sb("mask_sb", [P, S * S2], mybir.dt.uint8)
        flag = sb("flag", [P, 2])
        flag_tile = sb("flag_tile", [P, TILES])
        k_blk = sb("k_blk", [P, 2, HEADS, P])
        v_blk = sb("v_blk", [P, 2, BT, HG, OW])

        c_sb = sb("c_sb", [P, 2, BT, 2, GW])
        cl_sb = sb("cl_sb", [1, 2, BT, GW])
        st1 = sb("st1", [P, 2, 6])
        mv1 = sb("mv1", [P, 2, 2])
        rs1 = sb("rs1", [P, 2])
        ve1 = sb("ve1", [P, 2])
        x1 = sb("x1", [P, 2, D])
        x1b = sb("x1b", [P, TILES, D])
        x1t = sb("x1t", [P, 2, P])
        qt = sb("qt", [P, 2, P])
        g_sb = sb("g_sb", [P, 2, BT, GW])
        t_sb = sb("t_sb", [P, 2, BT, D])
        m_sb = sb("m_sb", [P, 2, BT, 32])
        vs_sb = sb("vs_sb", [P, 2, BT])
        rv_sb = sb("rv_sb", [P, 2, P])
        ct_sb = sb("ct_sb", [P, 2, P])
        y_sb = sb("y_sb", [P, 2, D])
        stn = sb("stn", [P, 2, 6])
        mvn = sb("mvn", [P, 2, 2])
        rsn = sb("rsn", [P, 2])
        ven = sb("ven", [P, 2])
        yn = sb("yn", [P, 2, D])
        fin = sb("fin", [P, 2, D])
        fin2 = sb("fin2", [P, 2, D])
        st2 = sb("st2", [P, 2, 6])
        mv2 = sb("mv2", [P, 2, 2])
        rs2 = sb("rs2", [P, 2])
        ve2 = sb("ve2", [P, 2])
        xn = sb("xn", [P, 2, D])
        xnt = sb("xnt", [P, 2, P])
        v_st = sb("v_st", [P, 2, D])
        qv = sb("qv", [P, 2, NB])
        pos_st = sb("pos_st", [P, 2, HEADS * S])
        pos_sb = sb("pos_sb", [P, 2, HEADS * S])
        v_rep = sb("v_rep", [P, 2, BT, D])
        qu = sb("qu", [P, 2, P])
        sc = sb("sc", [P, 2, HEADS * S])
        mx = sb("mx", [P, 2, HEADS])
        z_sb = sb("z_sb", [P, 2, HEADS * S])
        e_sb = sb("e_sb", [P, 2, HEADS * S])
        et = sb("et", [P, 2, HG, P])
        rden = sb("rden", [P, 2, HG, HG])
        cn = sb("cn", [P, 2, D])
        cnt = sb("cnt", [P, 2, P])
        x3 = sb("x3", [P, 2, D])
        x3t = sb("x3t", [P, 2, P])
        lg = sb("lg", [P, 2, EXPERTS])
        m8 = sb("m8", [P, 2, 8])
        dz = sb("dz", [P, 2])
        th = sb("th", [P, 2])
        g12 = sb("g12", [P, 2, 2])
        cmp_gt = sb("cmp_gt", [P, 2, EXPERTS, EXPERTS])
        cmp_eq = sb("cmp_eq", [P, 2, EXPERTS, EXPERTS])
        rank = sb("rank", [P, 2, EXPERTS])
        pick = sb("pick", [P, 2, 2, EXPERTS])
        gates = sb("gates", [P, 2, EXPERTS])
        sg = sb("sg", [P, 2, FF])
        sgg = sb("sgg", [P, 2, FR])
        hh = sb("hh", [P, 2, FF])
        ht = sb("ht", [P, 2, FF])

        bank = [ctx.enter_context(nc.psum_tensor(f"bank{n}", [P, 512], f32)) for n in range(8)]

        weights_in, x_in, mask_in = sem("weights_in"), sem("x_in"), sem("mask_in")
        ctx_in = [sem("ctx_in0"), sem("ctx_in1")]
        half_set, ones_set, last_ones_set, zeros_set = sem("half_set"), sem("ones_set"), sem("last_ones_set"), sem("zeros_set")
        cols_set, flag_set, ftile_set, poison_sum, poison_set = (
            sem("cols_set"), sem("flag_set"), sem("ftile_set"), sem("poison_sum"), sem("poison_set"))
        pos_keys, pos_blk_set, bk_set = sem("pos_keys"), sem("pos_blk_set"), sem("bk_set")
        st1_done, mv1_done, ve1_done, rs1_done, x1_done = (sem(n) for n in ("st1_done", "mv1_done", "ve1_done", "rs1_done", "x1_done"))
        x1b_done = sem("x1b_done")
        xt_ps, xt_done, qt_ps, qt_done, r_ps, g_ps, g_done = (
            sem(n) for n in ("xt_ps", "xt_done", "qt_ps", "qt_done", "r_ps", "g_ps", "g_done"))
        t_ps, t_done, vs_ps, vs_done, rv_done, m_ps, m_done = (
            sem(n) for n in ("t_ps", "t_done", "vs_ps", "vs_done", "rv_done", "m_ps", "m_done"))
        c_ps, ct_done, y_ps, y_done = (sem(n) for n in ("c_ps", "ct_done", "y_ps", "y_done"))
        stn_done, mvn_done, ven_done, rsn_done, yn_done, fin_mul, fin_add, x_new = (
            sem(n) for n in ("stn_done", "mvn_done", "ven_done", "rsn_done", "yn_done", "fin_mul", "fin_add", "x_new"))
        st2_done, mv2_done, ve2_done, rs2_done, xn_done = (sem(n) for n in ("st2_done", "mv2_done", "ve2_done", "rs2_done", "xn_done"))
        xnt_ps, xnt_done, qk_ps, q_done, k_done, v_ps, v_done = (
            sem(n) for n in ("xnt_ps", "xnt_done", "qk_ps", "q_done", "k_done", "v_ps", "v_done"))
        v_stored = [sem("v_stored0"), sem("v_stored1")]
        qv_done, p_ps, p_done = sem("qv_done"), sem("p_ps"), sem("p_done")
        pos_stored = [sem("pos_stored0"), sem("pos_stored1")]
        pos_in = [sem("pos_in0"), sem("pos_in1")]
        vrep_in = [sem("vrep_in0"), sem("vrep_in1")]
        kblk_in = [sem("kblk_in0"), sem("kblk_in1")]
        vblk_done, xb_done, qu_done, s_ps, sc_done, mx_done, z_done, e_done = (
            sem(n) for n in ("vblk_done", "xb_done", "qu_done", "s_ps", "sc_done", "mx_done", "z_done", "e_done"))
        et_ps, et_done, o_ps, rden_done, cn_done, cnt_ps, cnt_done, a_ps, x_att = (
            sem(n) for n in ("et_ps", "et_done", "o_ps", "rden_done", "cn_done", "cnt_ps", "cnt_done", "a_ps", "x_att"))
        st3_done, mv3_done, ve3_done, rs3_done, x3_done = (sem(n) for n in ("st3_done", "mv3_done", "ve3_done", "rs3_done", "x3_done"))
        x3t_ps, x3t_done, ab_ps, ffb_ps, sg_done = (sem(n) for n in ("x3t_ps", "x3t_done", "ab_ps", "ffb_ps", "sg_done"))
        lg_ps, lg_done, m8_done, dz_done, th_done, g12_done, gt_done, eq_done, eql_done, cmp_done, rank_done, pick_done, picked, gates_done = (
            sem(n) for n in ("lg_ps", "lg_done", "m8_done", "dz_done", "th_done", "g12_done", "gt_done", "eq_done",
                             "eql_done", "cmp_done", "rank_done", "pick_done", "picked", "gates_done"))
        sgg_done, h_done, ht_ps, ht_done, f_ps, x_out = (
            sem(n) for n in ("sgg_done", "h_done", "ht_ps", "ht_done", "f_ps", "x_out"))
        out_stored = [sem("out_stored0"), sem("out_stored1")]

        x_tok = x.rearrange("(t b) s d -> (b s) t d", b=BT)
        out_tok = out.rearrange("(t b) s d -> t (b s) d", b=BT)

        def at(buf, t):
            return buf[:, bass.ds(t, 1), :].rearrange("p o n -> p (o n)")

        def dram_at(ap, t):
            return ap[bass.ds(t, 1)].rearrange("o p n -> (o p) n")

        def pipeline(eng, step, depth):
            peel = depth + depth % 2
            for i in range(peel):
                step(i, i % 2, lambda k, i=i: i >= k)
            with eng.Fori(0, (TILES - peel) // 2) as pair:
                for slot in range(2):
                    step(2 * pair + (peel + slot), slot, lambda k: True)
            for i in range(TILES, TILES + depth):
                step(i, i % 2, lambda k, i=i: i - k < TILES)

        def tiles(eng, body):
            body(0, 0, True)
            body(1, 1, True)
            with eng.Fori(0, TILES // 2 - 1) as pair:
                for slot in range(2):
                    body(2 * pair + (2 + slot), slot, False)

        def loads_in(t, slot, n):
            return t * (8 * n) + (16 * n - 8 * n * slot)

        def cap(count):
            return min(count, TILES) if isinstance(count, int) else count

        def is_step(i, n):
            return isinstance(i, int) and i == n

        block = ctx.enter_context(nc.Block())

        @block.sync
        def _(sp):
            sp.dma_start(x_all[:], x_tok).then_inc(x_in, 16)
            sp.dma_start(w_sb[:], weights).then_inc(weights_in, 16)
            sp.dma_start(row_sb[:], rows.partition_broadcast(P)).then_inc(weights_in, 16)

            def load_context(i, slot, on):
                if on(0):
                    if on(2):
                        sp.wait_ge(g_ps, 2 * i - 2)
                    sp.dma_start(c_sb[:, slot, :, :, 0:D], ctx_main[bass.ds(i, 1)].rearrange("o p b c d -> (o p) b c d")).then_inc(ctx_in[slot], 16)
                    sp.dma_start(cl_sb[:, slot, :, 0:D], ctx_last[bass.ds(i, 1)]).then_inc(ctx_in[slot], 16)
                if is_step(i, 1):
                    sp.dma_start(mask_sb[:], mask).then_inc(mask_in, 16)
                if on(8):
                    sp.wait_ge(v_done, i - 7)
                    sp.dma_start(dram_at(v_scratch, i - 8), v_st[:, slot, :]).then_inc(v_stored[slot], 16)

            sp.wait_ge(ones_set, 1)
            sp.wait_ge(last_ones_set, 1)
            pipeline(sp, load_context, 8)

            with sp.Fori(0, S // 2) as pair:
                for slot in range(2):
                    i = 2 * pair + slot
                    sp.wait_ge(p_done, i + 3)
                    sp.dma_start(pos_scratch[:, bass.ds(i, 1), :].rearrange("b o n -> b (o n)"), pos_st[:, slot, :]).then_inc(pos_stored[slot], 16)

            for s in range(2):
                sp.wait_ge(v_stored[s], 16 * TILES // 2)
                sp.wait_ge(pos_stored[s], 16 * S // 2)
            sp.wait_ge(zeros_set, 2)
            pos_tok = pos_scratch.rearrange("(t b) i n -> t (b i) n", b=BT)
            v_tok = v_scratch.rearrange("t (b j) d -> t j b d", b=BT)

            def load_attention(t, slot, first):
                if not first:
                    sp.wait_ge(s_ps, t - 1)
                for h in range(HEADS):
                    sp.dma_start(k_blk[HD * h:HD * h + HD, slot, h, :],
                                 k_all[HD * h:HD * h + HD, bass.ds(t * P, P)]).then_inc(kblk_in[slot], 16)
                if not first:
                    sp.wait_ge(sc_done, t - 1)
                sp.dma_start(pos_sb[:, slot, :], dram_at(pos_tok, t)).then_inc(pos_in[slot], 16)
                if not first:
                    sp.wait_ge(vblk_done, t - 1)
                for h in range(HG):
                    sp.dma_start(v_rep[S * h:S * h + S, slot, :, :],
                                 v_tok[bass.ds(t, 1)].rearrange("o j b d -> (o j) b d")).then_inc(vrep_in[slot], 16)

            load_attention(0, 0, True)
            load_attention(1, 1, True)
            with sp.Fori(0, TILES // 2 - 1) as pair:
                for slot in range(2):
                    load_attention(2 * pair + (2 + slot), slot, False)

            with sp.Fori(0, TILES // 2) as pair:
                for slot in range(2):
                    t = 2 * pair + slot
                    sp.wait_ge(x_out, t + 1)
                    sp.dma_start(dram_at(out_tok, t), at(x_all, t)).then_inc(out_stored[slot], 16)
            for s in range(2):
                sp.wait_ge(out_stored[s], 16 * TILES // 2)

        @block.gpsimd
        def _(pool):
            pool.memset(half[:], -0.5).then_inc(half_set, 1)
            pool.memset(c_sb[:, :, :, :, D:GW], 1.0).then_inc(ones_set, 1)
            pool.memset(cl_sb[:, :, :, D:GW], 1.0).then_inc(last_ones_set, 1)
            pool.memset(k_blk[:, 0], 0.0).then_inc(zeros_set, 1)
            pool.memset(k_blk[:, 1], 0.0).then_inc(zeros_set, 1)
            pool.wait_ge(weights_in, 32)
            pool.wait_ge(x_in, 16)
            pool.wait_ge(half_set, 1)

            def cross(i, slot, on):
                if on(0) :
                    pool.wait_ge(ve1_done, i + 1)
                    pool.tensor_tensor(rs1[:, slot:slot + 1], ve1[:, slot:slot + 1], half[:], ALU.pow).then_inc(rs1_done, 1)
                if on(3):
                    pool.wait_ge(ven_done, i - 2)
                    s = (slot + 1) % 2
                    pool.tensor_tensor(rsn[:, s:s + 1], ven[:, s:s + 1], half[:], ALU.pow).then_inc(rsn_done, 1)
                if on(5):
                    pool.wait_ge(ve2_done, i - 4)
                    s = (slot + 1) % 2
                    pool.tensor_tensor(rs2[:, s:s + 1], ve2[:, s:s + 1], half[:], ALU.pow).then_inc(rs2_done, 1)
                if on(0):
                    pool.wait_ge(x1_done, i + 1)
                    pool.tensor_tensor(at(x1b, i), x1[:, slot, :], ROW("xbo"), ALU.add).then_inc(x1b_done, 1)
                if on(4):
                    pool.wait_ge(yn_done, i - 3)
                    pool.tensor_tensor(fin[:, slot, :], yn[:, slot, :], ROW("ln_g"), ALU.mult).then_inc(fin_mul, 1)
                if on(4):
                    pool.wait_ge(fin_mul, i - 3)
                    pool.tensor_tensor(fin2[:, slot, :], fin[:, slot, :], ROW("ln_b"), ALU.add).then_inc(fin_add, 1)
                    pool.wait_ge(fin_add, i - 3)
                    pool.tensor_tensor(at(x_all, i - 4), at(x_all, i - 4), fin2[:, slot, :], ALU.add).then_inc(x_new, 1)

            pipeline(pool, cross, 5)

            for s in range(2):
                pool.tensor_copy(v_blk[:, s, :, :, 32:OW].rearrange("p b g o -> p (b g) o"),
                                 W("ones4").unsqueeze(1).broadcast_to([P, BT * HG, 4])).then_inc(zeros_set, 1)

            pool.wait_ge(x_new, TILES)
            pool.wait_ge(xn_done, TILES)

            def spread(t, slot, first):
                pool.wait_ge(vrep_in[slot], loads_in(t, slot, HG))
                if not first:
                    pool.wait_ge(o_ps, t - 1)
                pool.tensor_tensor(v_blk[:, slot, :, :, 0:32], v_rep[:, slot, :, :].rearrange("p b (g n) -> p b g n", g=HG),
                                   W("vmask").unsqueeze(1).unsqueeze(1).broadcast_to([P, BT, HG, 32]), ALU.mult).then_inc(vblk_done, 1)
                pool.tensor_tensor(at(x_all, t), at(x_all, t), ROW("abo"), ALU.add).then_inc(xb_done, 1)

            tiles(pool, spread)

            def gate(i, slot, on):
                if on(0):
                    pool.wait_ge(ve3_done, i + 1)
                    pool.tensor_tensor(rs1[:, slot:slot + 1], ve1[:, slot:slot + 1], half[:], ALU.pow).then_inc(rs3_done, 1)
                if on(1):
                    s = (slot + 1) % 2
                    pool.wait_ge(sg_done, i)
                    pool.wait_ge(gates_done, i)
                    pool.tensor_tensor(sgg[:, s, :].rearrange("p (e n) -> p e n", e=EXPERTS), sg[:, s, 0:FR].rearrange("p (e n) -> p e n", e=EXPERTS),
                                       gates[:, s, :].unsqueeze(2).broadcast_to([P, EXPERTS, HID]), ALU.mult).then_inc(sgg_done, 1)

            pipeline(pool, gate, 1)

        @block.scalar
        def _(act):
            act.wait_ge(weights_in, 32)
            act.wait_ge(cols_set, 4)

            def cross(i, slot, on):
                if on(0):
                    act.wait_ge(xt_ps, i + 1)
                    act.activation(x1t[:, slot, :], bank[0][:, 0:P], ACT.Copy).then_inc(xt_done, 1)
                    if on(2):
                        act.wait_ge(vs_ps, i - 1)
                    act.wait_ge(g_ps, 2 * i + 1)
                    act.activation(g_sb[:, slot, 0:2, :], bank[2][:, 0:2 * GW].rearrange("p (b n) -> p b n", b=2), ACT.Copy).then_inc(g_done, 1)
                    if on(2):
                        act.wait_ge(c_ps, i - 1)
                    act.wait_ge(qt_ps, i + 1)
                    act.activation(qt[:, slot, :], bank[0][:, P:2 * P], ACT.Identity, bias=xbq_s, scale=1.0 / DK).then_inc(qt_done, 1)
                if on(5):
                    s = (slot + 1) % 2
                    if on(7):
                        act.wait_ge(v_ps, i - 6)
                        act.wait_ge(qk_ps, i - 6)
                    act.wait_ge(xnt_ps, i - 4)
                    act.activation(xnt[:, s, :], bank[7][:, 0:P], ACT.Identity, bias=W("beta"), scale=W("gamma")).then_inc(xnt_done, 1)
                if on(0):
                    act.wait_ge(g_ps, 2 * i + 2)
                    act.activation(g_sb[:, slot, 2:4, :], bank[3][:, 0:2 * GW].rearrange("p (b n) -> p b n", b=2), ACT.Copy).then_inc(g_done, 1)
                if on(5):
                    act.wait_ge(qk_ps, i - 4)
                    act.activation(q_all[:, bass.ds((i - 5) * BT, BT), :].rearrange("p b s -> p (b s)"), bank[7][:, P:2 * P], ACT.Copy).then_inc(q_done, 1)
                    act.activation(k_all[:, bass.ds((i - 5) * P, P)], bank[7][:, 2 * P:3 * P], ACT.Identity, bias=W("abk")).then_inc(k_done, 1)

            pipeline(act, cross, 7)

            act.wait_ge(q_done, TILES)
            with act.Fori(0, S // 2) as pair:
                for slot in range(2):
                    i = 2 * pair + slot
                    act.wait_ge(p_ps, i + 1)
                    act.activation(qv[:, slot, :], q_all[:, :, bass.ds(i, 1)].rearrange("p b o -> p (b o)"), ACT.Identity, bias=qv_b).then_inc(qv_done, 1)

            def attend(i, slot, on):
                if on(0):
                    if on(2):
                        act.wait_ge(s_ps, i - 1)
                    act.activation(qu[:, slot, :], q_all[:, bass.ds(i * BT, BT), :].rearrange("p b s -> p (b s)"), ACT.Identity, bias=qu_b).then_inc(qu_done, 1)
                if on(2):
                    act.wait_ge(z_done, i - 1)
                    if on(4):
                        act.wait_ge(et_ps, i - 3)
                    act.activation(e_sb[:, slot, :], z_sb[:, slot, :], ACT.Exp, scale=1.0 / math.sqrt(HD)).then_inc(e_done, 1)
                    act.wait_ge(et_ps, i - 1)
                    if on(4):
                        act.wait_ge(o_ps, i - 3)
                    act.activation(et[:, slot, :, :].rearrange("p g n -> p (g n)"), bank[2 + slot][:, :], ACT.Copy).then_inc(et_done, 1)
                if on(3):
                    s = (slot + 1) % 2
                    act.wait_ge(cnt_ps, i - 2)
                    if on(5):
                        act.wait_ge(a_ps, i - 4)
                    act.activation(cnt[:, s, :], bank[5][:, 0:P], ACT.Copy).then_inc(cnt_done, 1)

            pipeline(act, attend, 5)

            def feed(i, slot, on):
                if on(0):
                    act.wait_ge(x3t_ps, i + 1)
                    if on(2):
                        act.wait_ge(ffb_ps, i - 1)
                    act.activation(x3t[:, slot, :], bank[6][:, 0:P], ACT.Copy).then_inc(x3t_done, 1)
                    if on(2):
                        act.wait_ge(h_done, i - 1)
                        act.wait_ge(sgg_done, i - 1)
                    act.wait_ge(ab_ps, i + 1)
                    act.activation(sg[:, slot, 0:FR], bank[0][:, :], ACT.Silu)
                    act.wait_ge(ffb_ps, i + 1)
                    act.activation(sg[:, slot, FR:FF], bank[2 + 2 * slot][:, 0:FS], ACT.Silu).then_inc(sg_done, 1)
                    act.wait_ge(dz_done, i + 1)
                    act.activation(th[:, slot:slot + 1], dz[:, slot:slot + 1], ACT.Tanh, scale=0.5).then_inc(th_done, 1)
                if on(1):
                    s = (slot + 1) % 2
                    act.wait_ge(ht_ps, i)
                    if on(3):
                        act.wait_ge(f_ps, i - 2)
                    act.activation(ht[:, s, 0:512], bank[3][:, :], ACT.Copy)
                    act.activation(ht[:, s, 512:FF], bank[5][:, P:2 * P], ACT.Copy).then_inc(ht_done, 1)

            pipeline(act, feed, 3)

        @block.vector
        def _(dve):
            dve.wait_ge(weights_in, 32)
            dve.tensor_scalar(xbq_s, W("xbq"), 1.0 / DK, None, ALU.mult).then_inc(cols_set, 1)
            dve.tensor_scalar(xbv_n, W("xbv"), float(S2), None, ALU.mult).then_inc(cols_set, 1)
            dve.tensor_tensor(qu_b, W("abq"), W("u"), ALU.add).then_inc(cols_set, 1)
            dve.tensor_tensor(qv_b, W("abq"), W("v"), ALU.add).then_inc(cols_set, 1)
            dve.tensor_scalar(bk_heads[:], W("blk128"), W("xbk"), None, ALU.mult).then_inc(bk_set, 1)
            dve.wait_ge(pos_keys, 1)
            dve.tensor_tensor(pos_blk[:], bank[1][:, 0:POS].unsqueeze(1).broadcast_to([P, HEADS, POS]),
                              W("head16").unsqueeze(2).broadcast_to([P, HEADS, POS]), ALU.mult).then_inc(pos_blk_set, 1)
            dve.wait_ge(x_in, 16)
            dve.wait_ge(cols_set, 4)

            def moments(slot, src, stat, mv, ve, st_sem, mv_sem, ve_sem, count, scale, eps):
                dve.bn_stats(stat[:, slot, :], src).then_inc(st_sem, 1)
                dve.wait_ge(st_sem, count)
                dve.nop(nofuse=True)
                dve.bn_aggr(mv[:, slot, :], stat[:, slot, :]).then_inc(mv_sem, 1)
                dve.wait_ge(mv_sem, count)
                dve.tensor_scalar(ve[:, slot:slot + 1], mv[:, slot, 1:2], scale, eps, ALU.mult, ALU.add).then_inc(ve_sem, 1)

            def mask_flags():
                dve.wait_ge(mask_in, 16)
                dve.tensor_reduce(flag[:, 0:1], mask_sb[:].bitcast(mybir.dt.int32), AX, ALU.max).then_inc(flag_set, 1)
                dve.wait_ge(flag_set, 1)
                dve.tensor_scalar(flag[:, 1:2], flag[:, 0:1], 0.0, None, ALU.is_gt).then_inc(flag_set, 1)
                dve.wait_ge(flag_set, 2)
                dve.tensor_scalar(flag_tile[:], W("batch_tile"), flag[:, 1:2], None, ALU.mult).then_inc(ftile_set, 1)

            def mask_poison():
                dve.wait_ge(poison_sum, 1)
                dve.tensor_scalar(poison[:], bank[6][:, 0:TILES], -3.0e38, 3.0e38, ALU.mult, ALU.mult).then_inc(poison_set, 1)
                dve.wait_ge(poison_set, 1)

            def cross(i, slot, on):
                other = (slot + 1) % 2
                if on(0):
                    moments(slot, at(x_all, i), st1, mv1, ve1, st1_done, mv1_done, ve1_done, i + 1, 1.0, EPS)
                if on(5):
                    dve.wait_ge(x_new, i - 4)
                    moments(other, at(x_all, i - 5), st2, mv2, ve2, st2_done, mv2_done, ve2_done, i - 4, 1.0 + EPS, EPS * EPS)
                if is_step(i, 3):
                    mask_poison()
                if on(3):
                    dve.wait_ge(y_ps, i - 2)
                    dve.wait_ge(x1b_done, i - 2)
                    dve.scalar_tensor_tensor(y_sb[:, other, :], bank[6][:, 0:D], poison[:, bass.ds(i - 3, 1)], at(x1b, i - 3),
                                             ALU.add, ALU.add).then_inc(y_done, 1)
                    dve.wait_ge(y_done, i - 2)
                    moments(other, y_sb[:, other, :], stn, mvn, ven, stn_done, mvn_done, ven_done, i - 2, 1.0, EPS)
                if on(2):
                    dve.wait_ge(m_ps, i - 1)
                    dve.tensor_tensor(m_sb[:, slot, :, :], bank[5][:, 0:BT * 32].rearrange("p (b n) -> p b n", b=BT),
                                      W("blk32").unsqueeze(1).broadcast_to([P, BT, 32]), ALU.mult).then_inc(m_done, 1)
                if on(1):
                    dve.wait_ge(t_ps, i)
                    for b in range(BT):
                        dve.scalar_tensor_tensor(t_sb[:, other, b, :], ROW("xbv"), g_sb[:, other, b, D:GW],
                                                 bank[4][:, b * D:(b + 1) * D], ALU.mult, ALU.add).then_inc(t_done, 1)
                if on(6):
                    dve.wait_ge(v_ps, i - 5)
                    if on(8):
                        dve.wait_ge(v_stored[slot], loads_in(i - 8, slot, 1))
                    dve.tensor_tensor(v_st[:, slot, :], bank[6][:, P:2 * P], ROW("abv"), ALU.add).then_inc(v_done, 1)
                if on(1):
                    dve.wait_ge(vs_ps, i)
                    dve.tensor_scalar(vs_sb[:, other, :], bank[1][:, P:P + BT], xbv_n, None, ALU.add).then_inc(vs_done, 1)
                if on(2):
                    dve.wait_ge(c_ps, i - 1)
                    dve.wait_ge(rv_done, i - 1)
                    dve.tensor_tensor(ct_sb[:, slot, :], bank[5][:, P:2 * P], rv_sb[:, slot, :], ALU.add).then_inc(ct_done, 1)
                if on(1):
                    dve.wait_ge(vs_done, i)
                    dve.wait_ge(r_ps, i)
                    dve.tensor_tensor(rv_sb[:, other, :].rearrange("p (b s) -> p b s", b=BT), bank[1][:, 0:P].rearrange("p (b s) -> p b s", b=BT),
                                      vs_sb[:, other, :].unsqueeze(2).broadcast_to([P, BT, S]), ALU.mult).then_inc(rv_done, 1)
                if on(0):
                    if on(2):
                        dve.wait_ge(xt_ps, i - 1)
                        dve.wait_ge(x1b_done, i - 1)
                    dve.wait_ge(rs1_done, i + 1)
                    dve.tensor_scalar(x1[:, slot, :], at(x_all, i), mv1[:, slot, 0:1], rs1[:, slot:slot + 1], ALU.subtract, ALU.mult).then_inc(x1_done, 1)
                if on(3):
                    if on(5):
                        dve.wait_ge(fin_mul, i - 4)
                    dve.wait_ge(rsn_done, i - 2)
                    dve.tensor_scalar(yn[:, other, :], y_sb[:, other, :], mvn[:, other, 0:1], rsn[:, other:other + 1], ALU.subtract, ALU.mult).then_inc(yn_done, 1)
                if on(5):
                    if on(7):
                        dve.wait_ge(xnt_ps, i - 6)
                    dve.wait_ge(rs2_done, i - 4)
                    dve.tensor_scalar(xn[:, other, :], at(x_all, i - 5), mv2[:, other, 0:1], rs2[:, other:other + 1], ALU.subtract, ALU.mult).then_inc(xn_done, 1)
                if is_step(i, 1):
                    mask_flags()

            pipeline(dve, cross, 8)

            dve.sem_inc(p_done, 2)

            def keep_positions(i, slot, first):
                dve.wait_ge(p_ps, i + 3)
                if not first:
                    dve.wait_ge(pos_stored[slot], loads_in(i - 2, slot, 1))
                dve.tensor_copy(pos_st[:, slot, :], bank[slot][:, :]).then_inc(p_done, 1)

            tiles(dve, keep_positions)

            def heads(ap):
                return ap.rearrange("p (h j) -> p h j", h=HEADS)

            def attend(i, slot, on):
                other = (slot + 1) % 2
                if on(0):
                    dve.wait_ge(s_ps, i + 1)
                    dve.wait_ge(pos_in[slot], loads_in(i, slot, 1))
                    dve.tensor_tensor(sc[:, slot, :], bank[slot][:, :], pos_sb[:, slot, :], ALU.add).then_inc(sc_done, 1)
                if on(2):
                    dve.wait_ge(o_ps, i - 1)
                    dve.reciprocal(rden[:, slot, :, :], bank[4][:, 0:HG * OW].rearrange("p (g n) -> p g n", g=HG)[:, :, 32:OW]).then_inc(rden_done, 1)
                if on(0):
                    dve.wait_ge(sc_done, i + 1)
                    dve.tensor_reduce(mx[:, slot, :], heads(sc[:, slot, :]), AX, ALU.max).then_inc(mx_done, 1)
                if on(2):
                    dve.wait_ge(rden_done, i - 1)
                    if on(4):
                        dve.wait_ge(cnt_ps, i - 3)
                    dve.tensor_tensor(cn[:, slot, :].rearrange("p (g h n) -> p g h n", g=HG, h=HG),
                                      bank[4][:, 0:HG * OW].rearrange("p (g n) -> p g n", g=HG)[:, :, 0:32].rearrange("p g (h n) -> p g h n", h=HG),
                                      rden[:, slot, :, :].unsqueeze(3).broadcast_to([P, HG, HG, HD]), ALU.mult).then_inc(cn_done, 1)
                if on(0):
                    dve.wait_ge(mx_done, i + 1)
                    if on(2):
                        dve.wait_ge(e_done, i - 1)
                    dve.tensor_tensor(heads(z_sb[:, slot, :]), heads(sc[:, slot, :]),
                                      mx[:, slot, :].unsqueeze(2).broadcast_to([P, HEADS, S]), ALU.subtract).then_inc(z_done, 1)
                if on(3):
                    dve.wait_ge(a_ps, i - 2)
                    dve.wait_ge(xb_done, i - 2)
                    dve.tensor_tensor(at(x_all, i - 3), bank[6][:, 0:D], at(x_all, i - 3), ALU.add).then_inc(x_att, 1)

            pipeline(dve, attend, 4)

            def feed(i, slot, on):
                other = (slot + 1) % 2
                if on(0):
                    dve.wait_ge(x_att, i + 1)
                    if on(1):
                        dve.wait_ge(rs3_done, i)
                    moments(slot, at(x_all, i), st1, mv1, ve1, st3_done, mv3_done, ve3_done, i + 1, 1.0, EPS)
                if on(3):
                    dve.wait_ge(f_ps, i - 2)
                    dve.tensor_tensor(at(x_all, i - 3), bank[5][:, 0:D], at(x_all, i - 3), ALU.add).then_inc(x_out, 1)
                if on(1):
                    L = lg[:, other, :]
                    dve.wait_ge(lg_ps, i)
                    dve.tensor_tensor(L, bank[6][:, P:P + EXPERTS], ROW("rb"), ALU.add).then_inc(lg_done, 1)
                    dve.wait_ge(lg_done, i)
                    dve.nop(nofuse=True)
                    dve.max(m8[:, other, :], L).then_inc(m8_done, 1)
                    mine = L.unsqueeze(2).broadcast_to([P, EXPERTS, EXPERTS])
                    theirs = L.unsqueeze(1).broadcast_to([P, EXPERTS, EXPERTS])
                    dve.tensor_tensor(cmp_gt[:, other], theirs, mine, ALU.is_gt).then_inc(gt_done, 1)
                    dve.wait_ge(m8_done, i)
                    dve.tensor_tensor(dz[:, other:other + 1], m8[:, other, 0:1], m8[:, other, 1:2], ALU.subtract).then_inc(dz_done, 1)
                    dve.tensor_tensor(cmp_eq[:, other], theirs, mine, ALU.is_equal).then_inc(eq_done, 1)
                    dve.wait_ge(eq_done, i)
                    dve.tensor_tensor(cmp_eq[:, other], cmp_eq[:, other], W("lower").rearrange("p (a b) -> p a b", a=EXPERTS), ALU.mult).then_inc(eql_done, 1)
                    dve.wait_ge(eql_done, i)
                    dve.wait_ge(gt_done, i)
                    dve.tensor_tensor(cmp_gt[:, other], cmp_gt[:, other], cmp_eq[:, other], ALU.add).then_inc(cmp_done, 1)
                    dve.wait_ge(cmp_done, i)
                    dve.tensor_reduce(rank[:, other, :], cmp_gt[:, other], AX, ALU.add).then_inc(rank_done, 1)
                    dve.wait_ge(th_done, i)
                    dve.tensor_scalar(g12[:, other, 0:1], th[:, other:other + 1], 0.5, 0.5, ALU.mult, ALU.add)
                    dve.tensor_scalar(g12[:, other, 1:2], th[:, other:other + 1], -0.5, 0.5, ALU.mult, ALU.add).then_inc(g12_done, 1)
                    dve.wait_ge(rank_done, i)
                    dve.wait_ge(g12_done, i)
                    for r in range(2):
                        dve.tensor_scalar(pick[:, other, r, :], rank[:, other, :], float(r), g12[:, other, r:r + 1], ALU.is_equal, ALU.mult).then_inc(pick_done, 1)
                    dve.wait_ge(pick_done, 2 * i)
                    if on(3):
                        dve.wait_ge(sgg_done, i - 2)
                    dve.tensor_tensor(gates[:, other, :], pick[:, other, 0, :], pick[:, other, 1, :], ALU.add).then_inc(gates_done, 1)
                if on(0):
                    if on(2):
                        dve.wait_ge(x3t_ps, i - 1)
                    dve.wait_ge(rs3_done, i + 1)
                    dve.tensor_scalar(x3[:, slot, :], at(x_all, i), mv1[:, slot, 0:1], rs1[:, slot:slot + 1], ALU.subtract, ALU.mult).then_inc(x3_done, 1)
                if on(1):
                    if on(3):
                        dve.wait_ge(ht_ps, i - 2)
                    dve.wait_ge(sg_done, i)
                    dve.tensor_tensor(hh[:, other, FR:FF], bank[2 + 2 * other][:, FS:2 * FS], sg[:, other, FR:FF], ALU.mult)
                    dve.wait_ge(sgg_done, i)
                    dve.tensor_tensor(hh[:, other, 0:FR], bank[1 + 6 * other][:, :], sgg[:, other, :], ALU.mult).then_inc(h_done, 1)

            pipeline(dve, feed, 3)

        @block.tensor
        def _(pe):
            pe.wait_ge(weights_in, 32)
            mm = nc.tensor.matmul
            ident = W("ident")
            mm(bank[1][:, 0:POS], W("awp"), W("pe"), start=True, stop=True).then_inc(pos_keys, 1)
            pe.wait_ge(pos_blk_set, 1)
            pe.wait_ge(bk_set, 1)

            def cross(j, slot, on):
                other = (slot + 1) % 2

                def gram(half):
                    g = bank[2 + half]
                    for n in range(2):
                        b = 2 * half + n
                        o = g[:, n * GW:(n + 1) * GW]
                        mm(o, c_sb[:, slot, b, 0, 0:D], c_sb[:, slot, b, 0, :], start=True, stop=False)
                        mm(o, c_sb[:, slot, b, 1, 0:D], c_sb[:, slot, b, 1, :], start=False, stop=False)
                        last = mm(o, cl_sb[:, slot, b, 0:D], cl_sb[:, slot, b, :], start=False, stop=True)
                    last.then_inc(g_ps, 1)

                if on(0):
                    pe.wait_ge(x1_done, j + 1)
                    nc.tensor.transpose(bank[0][:, 0:P], x1[:, slot, :], ident).then_inc(xt_ps, 1)
                    pe.wait_ge(ctx_in[slot], loads_in(j, slot, 2))
                    gram(0)
                    pe.wait_ge(xt_done, j + 1)
                    mm(bank[0][:, P:2 * P], W("xwq"), x1t[:, slot, :], start=True, stop=True).then_inc(qt_ps, 1)
                if on(5):
                    if on(6):
                        pe.wait_ge(k_done, j - 5)
                    pe.wait_ge(xn_done, j - 4)
                    nc.tensor.transpose(bank[7][:, 0:P], xn[:, other, :], ident).then_inc(xnt_ps, 1)
                if on(2):
                    if on(6):
                        pe.wait_ge(v_done, j - 5)
                    if is_step(j, 2):
                        pe.wait_ge(ftile_set, 1)
                        mm(bank[6][:, 0:TILES], W("batch_row"), flag_tile[:], start=True, stop=True).then_inc(poison_sum, 1)
                        pe.wait_ge(poison_set, 1)
                    pe.wait_ge(ct_done, j - 1)
                    mm(bank[6][:, 0:D], ct_sb[:, slot, :], W("xwo"), start=True, stop=True).then_inc(y_ps, 1)
                if on(0):
                    gram(1)
                    pe.wait_ge(qt_done, j + 1)
                    if on(1):
                        pe.wait_ge(rv_done, j)
                    mm(bank[1][:, 0:P], bk_heads[:], qt[:, slot, :], start=True, stop=True).then_inc(r_ps, 1)
                if on(5):
                    pe.wait_ge(xnt_done, j - 4)
                    mm(bank[7][:, P:2 * P], W("awq"), xnt[:, other, :], start=True, stop=True)
                    mm(bank[7][:, 2 * P:3 * P], W("awk"), xnt[:, other, :], start=True, stop=True).then_inc(qk_ps, 1)
                    pe.wait_ge(y_done, cap(j - 1))
                    mm(bank[6][:, P:2 * P], xnt[:, other, :], W("awv"), start=True, stop=True).then_inc(v_ps, 1)
                if on(1):
                    if on(2):
                        pe.wait_ge(ct_done, j - 1)
                    pe.wait_ge(t_done, BT * j)
                    for g in range(HG):
                        last = mm(bank[5][32 * g:32 * g + 32, 0:BT * 32].rearrange("p (b n) -> p b n", b=BT), W("xwk")[:, 32 * g:32 * g + 32],
                                  t_sb[:, other, :, 32 * g:32 * g + 32], start=True, stop=True)
                    last.then_inc(m_ps, 1)
                if on(0):
                    for b in range(BT):
                        if b % 2 == 0:
                            pe.wait_ge(g_done, 2 * j + 1 + b // 2)
                        last = mm(bank[4][:, b * D:(b + 1) * D], g_sb[:, slot, b, 0:D], W("xwv"), start=True, stop=True)
                    last.then_inc(t_ps, 1)
                    mm(bank[1][:, P:P + BT], W("xwv"), g_sb[:, slot, :, D], start=True, stop=True).then_inc(vs_ps, 1)
                if on(1):
                    pe.wait_ge(m_done, j)
                    pe.nop(nofuse=True)
                    for b in range(BT):
                        for g in range(HG):
                            r = slice(32 * g, 32 * g + 32)
                            last = mm(bank[5][r, P + S * b:P + S * b + S], m_sb[r, other, b, :], qt[r, other, S * b:S * b + S], start=True, stop=True)
                    last.then_inc(c_ps, 1)

            pipeline(pe, cross, 5)

            pe.sem_inc(p_ps, 2)
            pe.wait_ge(ct_done, TILES)
            with pe.Fori(0, S // 2) as pair:
                for slot in range(2):
                    i = 2 * pair + slot
                    pe.wait_ge(qv_done, i + 1)
                    pe.wait_ge(p_done, i + 1)
                    pe.nop(nofuse=True)
                    mm(bank[slot][:, :].rearrange("p (h j) -> p h j", h=HEADS), qv[:, slot, :], pos_blk[:, :, bass.ds((S - 1 - slot) - 2 * pair, S)],
                       start=True, stop=True).then_inc(p_ps, 1)

            pe.wait_ge(p_done, S + 2)
            pe.wait_ge(v_done, TILES)

            def attend(j, slot, on):
                other = (slot + 1) % 2
                if on(0):
                    pe.wait_ge(qu_done, j + 1)
                    pe.wait_ge(kblk_in[slot], loads_in(j, slot, HEADS))
                    if on(2):
                        pe.wait_ge(sc_done, j - 1)
                    for b in range(BT):
                        last = mm(bank[slot][S * b:S * b + S, :].rearrange("p (h j) -> p h j", h=HEADS), qu[:, slot, S * b:S * b + S],
                                  k_blk[:, slot, :, S * b:S * b + S], start=True, stop=True)
                    last.then_inc(s_ps, 1)
                if on(2):
                    pe.wait_ge(et_done, j - 1)
                    pe.wait_ge(vblk_done, j - 1)
                    if on(3):
                        pe.wait_ge(cn_done, j - 2)
                    for g in range(HG):
                        for b in range(BT):
                            last = mm(bank[4][S * b:S * b + S, g * OW:(g + 1) * OW], et[:, slot, g, S * b:S * b + S],
                                      v_blk[:, slot, b, g, :], start=True, stop=True)
                    last.then_inc(o_ps, 1)
                if on(1):
                    pe.wait_ge(e_done, j)
                    if on(3):
                        pe.wait_ge(et_done, j - 2)
                    for g in range(HG):
                        last = nc.tensor.transpose(bank[2 + other][:, g * P:(g + 1) * P], e_sb[:, other, g * P:(g + 1) * P], ident)
                    last.then_inc(et_ps, 1)
                if on(2):
                    pe.wait_ge(cn_done, j - 1)
                    if on(3):
                        pe.wait_ge(cnt_done, j - 2)
                    nc.tensor.transpose(bank[5][:, 0:P], cn[:, slot, :], ident).then_inc(cnt_ps, 1)
                if on(3):
                    pe.wait_ge(cnt_done, j - 2)
                    if on(4):
                        pe.wait_ge(x_att, j - 3)
                    mm(bank[6][:, 0:D], cnt[:, other, :], W("awo"), start=True, stop=True).then_inc(a_ps, 1)

            pipeline(pe, attend, 3)

            pe.wait_ge(x_att, TILES)

            def feed(j, slot, on):
                other = (slot + 1) % 2
                if on(0):
                    pe.wait_ge(x3_done, j + 1)
                    if on(1):
                        pe.wait_ge(lg_done, j)
                    nc.tensor.transpose(bank[6][:, 0:P], x3[:, slot, :], ident).then_inc(x3t_ps, 1)
                if on(2):
                    pe.wait_ge(ht_done, j - 1)
                    if on(3):
                        pe.wait_ge(x_out, j - 2)
                    for c in range(CHUNKS):
                        last = mm(bank[5][:, 0:D], ht[:, slot, c * P:(c + 1) * P], W("w2")[:, c * D:(c + 1) * D],
                                  start=(c == 0), stop=(c == CHUNKS - 1))
                    last.then_inc(f_ps, 1)
                if on(0):
                    pe.wait_ge(x3t_done, j + 1)
                    if on(2):
                        pe.wait_ge(h_done, j - 1)
                    mm(bank[6][:, P:P + EXPERTS], x3t[:, slot, :], W("router"), start=True, stop=True).then_inc(lg_ps, 1)
                    if on(1):
                        pe.wait_ge(sg_done, j)
                    mm(bank[0][:, :], x3t[:, slot, :], W("w1")[:, 0:FR], start=True, stop=True).then_inc(ab_ps, 1)
                    mm(bank[1 + 6 * slot][:, :], x3t[:, slot, :], W("w3")[:, 0:FR], start=True, stop=True)
                    mm(bank[2 + 2 * slot][:, 0:FS], x3t[:, slot, :], W("w1")[:, FR:FF], start=True, stop=True)
                    mm(bank[2 + 2 * slot][:, FS:2 * FS], x3t[:, slot, :], W("w3")[:, FR:FF], start=True, stop=True).then_inc(ffb_ps, 1)
                if on(1):
                    pe.wait_ge(h_done, j)
                    if on(2):
                        pe.wait_ge(ht_done, j - 1)
                        pe.wait_ge(x_out, j - 1)
                    for c in range(CHUNKS):
                        o = bank[3][:, c * P:(c + 1) * P] if c < 4 else bank[5][:, P:2 * P]
                        last = nc.tensor.transpose(o, hh[:, other, c * P:(c + 1) * P], ident)
                    last.then_inc(ht_ps, 1)

            pipeline(pe, feed, 2)


def position_table():
    pos = np.arange(S, dtype=np.float32)[:, None]
    div = np.exp(np.arange(0, D, 2, dtype=np.float32) * np.float32(-math.log(10000.0) / D)).astype(np.float32)
    ang = pos * div
    plus = np.stack([np.sin(ang), np.cos(ang)], axis=-1).reshape(S, D)
    minus = np.stack([np.sin(-ang), np.cos(-ang)], axis=-1).reshape(S, D)
    return np.concatenate([plus[::-1], minus[1:]], axis=0).astype(np.float32)


def shape_tables():
    p = np.arange(P)
    f = lambda a: np.ascontiguousarray(a, dtype=np.float32)
    e = np.arange(EXPERTS)
    return {
        "pe": f(position_table().T),
        "ident": f(np.eye(P)),
        "blk32": f((p[:, None] % 32) // HD == np.arange(32)[None] // HD),
        "blk128": f(p[:, None] // HD == p[None] // HD),
        "head16": f(p[:, None] // HD == np.arange(HEADS)[None]),
        "vmask": f(p[:, None] // S == np.arange(32)[None] // HD),
        "ones4": f(p[:, None] // S == np.arange(4)[None]),
        "batch_row": f(p[:, None] % BT == p[None] // S),
        "batch_tile": f(p[:, None] // BT == np.arange(TILES)[None]),
        "lower": f(np.broadcast_to((e[None, :] < e[:, None]).reshape(1, -1), (P, EXPERTS * EXPERTS))),
    }


def kernel(**inputs):
    import concourse.bacc as bacc
    from concourse.bass_utils import run_bass_kernel_spmd

    a = {k: np.asarray(v) for k, v in inputs.items()}
    X, A, F = "L0_xattn_", "L0_attn_", "L0_ffn_"

    def experts(name):
        return np.concatenate([a[F + "routed_" + name].transpose(1, 0, 2).reshape(D, FR),
                               a[F + "shared_" + name].transpose(1, 0, 2).reshape(D, FS)], axis=1)

    w2 = np.concatenate([a[F + "routed_w2"].reshape(FR, D), a[F + "shared_w2"].reshape(FS, D)], axis=0)
    col = lambda name: a[name].reshape(P, 1)
    parts = {
        "xwq": a[X + "wq_w"].T, "xwk": a[X + "wk_w"].T, "xwv": a[X + "wv_w"].T, "xwo": a[X + "wo_w"].T,
        "awq": a[A + "Wq"].T, "awk": a[A + "Wk"].T, "awv": a[A + "Wv"].T, "awp": a[A + "Wpos"].T, "awo": a[A + "Wout"].T,
        "w1": experts("w1"), "w3": experts("w3"),
        "w2": w2.reshape(CHUNKS, P, D).transpose(1, 0, 2).reshape(P, FF), "router": a[F + "router_w"],
        "xbq": col(X + "wq_b"), "xbk": col(X + "wk_b"), "xbv": col(X + "wv_b"), "abq": col(A + "bq"), "abk": col(A + "bk"),
        "u": col(A + "u_bias"), "v": col(A + "v_bias"), "gamma": col(A + "ln_gamma"), "beta": col(A + "ln_beta"),
        **shape_tables(),
    }
    weights = np.ascontiguousarray(np.concatenate([parts[n] for n, _ in WEIGHT_BLOCKS], axis=1))
    vectors = {"xbv": a[X + "wv_b"], "xbo": a[X + "wo_b"], "ln_g": a[X + "ln_g"], "ln_b": a[X + "ln_b"],
               "abv": a[A + "bv"], "abo": a[A + "bout"], "rb": a[F + "router_b"]}
    rows = np.ascontiguousarray(np.concatenate([vectors[n] for n, _ in ROW_BLOCKS]))
    c = a["ctx_1024"]
    ctx_main = np.ascontiguousarray(c[:, :2 * P].reshape(TILES, BT, 2, P, D).transpose(0, 3, 1, 2, 4))
    ctx_last = np.ascontiguousarray(c[:, 2 * P].reshape(TILES, BT, D))
    mask = np.ascontiguousarray(a["mask_Bx1xSxS2_bf0"]).reshape(NB, S * S2)
    arrays = {"in_x": np.ascontiguousarray(a["x"]), "in_ctx_main": ctx_main, "in_ctx_last": ctx_last,
              "in_mask": mask, "in_weights": weights, "in_rows": rows}

    nc = bacc.Bacc("TRN2", target_bir_lowering=False, num_devices=1)
    f32 = mybir.dt.float32
    args = [nc.dram_tensor(n, v.shape, mybir.dt.from_np(v.dtype), kind="ExternalInput").ap() for n, v in arrays.items()]
    out = nc.dram_tensor("out_x", (NB, S, D), f32, kind="ExternalOutput").ap()
    pos_scratch = nc.dram_tensor("pos_scratch", (NB, S, HEADS * S), f32, kind="Internal").ap()
    v_scratch = nc.dram_tensor("v_scratch", (TILES, P, D), f32, kind="Internal").ap()
    perceiver_kernel(nc, *args, out, pos_scratch, v_scratch)
    r = run_bass_kernel_spmd(nc, [arrays], core_ids=[0])
    return r.results[0]["out_x"]
```

```python
import math

import numpy as np

import concourse.bass as bass
from concourse import mybir

NB, S, D = 128, 32, 128
S2 = 257
ARENA = 13900
HEADS, HD = 16, 8
P = 128
BT = P // S
TILES = NB // BT
GT = 4
HG = P // S
POS = 2 * S - 1
EXPERTS, HID, SHARED = 8, 64, 2
FR, FS = EXPERTS * HID, SHARED * HID
FF = FR + FS
CHUNKS = FF // P
EPS = 1e-5
DK = float(np.float32(np.sqrt(np.float16(HD))) + np.float32(1e-8))
GW = D + 1
OW = 36

WEIGHT_BLOCKS = [
    ("xwq", D), ("xwk", D), ("xwv", D), ("xwo", D),
    ("awq", D), ("awk", D), ("awv", D), ("awp", D), ("awo", D),
    ("w1", FF), ("w3", FF), ("w2", FF), ("router", EXPERTS),
    ("xbq", 1), ("xbk", 1), ("xbv", 1), ("abq", 1), ("abk", 1), ("u", 1), ("v", 1), ("gamma", 1), ("beta", 1),
    ("pe", POS), ("ident", P), ("blk32", 32), ("blk128", P), ("head16", HEADS), ("vmask", 32), ("ones4", 4),
    ("batch_row", P), ("batch_tile", TILES), ("lower", EXPERTS * EXPERTS),
]
ROW_BLOCKS = [("xbv", D), ("xbo", D), ("ln_g", D), ("ln_b", D), ("abv", D), ("abo", D), ("rb", EXPERTS)]


def offsets(blocks):
    at, out = 0, {}
    for name, n in blocks:
        out[name] = (at, n)
        at += n
    return out, at


WEIGHT_AT, WEIGHT_COLS = offsets(WEIGHT_BLOCKS)
ROW_AT, ROW_COLS = offsets(ROW_BLOCKS)


def perceiver_kernel(nc, x, ctx_main, ctx_last, mask, weights, rows, out, pos_scratch, v_scratch):
    f32 = mybir.dt.float32
    ALU = mybir.AluOpType
    ACT = mybir.ActivationFunctionType
    AX = mybir.AxisListType.X

    from contextlib import ExitStack

    ctx = ExitStack()
    with ctx:
        def sb(name, shape, dt=f32):
            return ctx.enter_context(nc.sbuf_tensor(name, shape, dt))

        def sem(name):
            return ctx.enter_context(nc.semaphore(name))

        w_sb = sb("w_sb", [P, WEIGHT_COLS])
        row_sb = sb("row_sb", [P, ROW_COLS])

        def W(name):
            at, n = WEIGHT_AT[name]
            return w_sb[:, at:at + n]

        def ROW(name):
            at, n = ROW_AT[name]
            return row_sb[:, at:at + n]

        x_all = sb("x_all", [P, TILES, D])
        q_all = sb("q_all", [P, NB, S])
        k_all = sb("k_all", [P, NB * S])
        half = sb("half", [P, 1])
        poison = sb("poison", [P, TILES])
        cols = sb("cols", [P, 8])
        xbq_s, xbv_n, qu_b, qv_b = (cols[:, n:n + 1] for n in range(4))
        bk_heads = sb("bk_heads", [P, P])
        pos_blk = sb("pos_blk", [P, HEADS, POS])
        mask_sb = sb("mask_sb", [P, S * S2], mybir.dt.uint8)
        flag = sb("flag", [P, 2])
        flag_tile = sb("flag_tile", [P, TILES])
        k_blk = sb("k_blk", [P, 2, HEADS, GT * P])
        v_blk = sb("v_blk", [P, 2, BT, HG, OW])

        arena = sb("arena", [P, ARENA])

        def phase():
            at = [0]

            def part(name, shape):
                n = int(np.prod(shape[1:]))
                assert at[0] + n <= ARENA, name
                flat = arena[0:shape[0], at[0]:at[0] + n]
                at[0] += n
                names = [f"d{k}" for k in range(len(shape) - 1)]
                if len(names) == 1:
                    return flat
                return flat.rearrange(f"p ({' '.join(names)}) -> p {' '.join(names)}", **dict(zip(names[1:], shape[2:])))
            return part

        cross_part, attend_part, feed_part = phase(), phase(), phase()

        c_sb = cross_part("c_sb", [P, 2, BT, 2, GW])
        cl_sb = cross_part("cl_sb", [1, 2, BT, GW])
        st1 = cross_part("st1", [P, 2, 6])
        mv1 = cross_part("mv1", [P, 2, 2])
        rs1 = cross_part("rs1", [P, 2])
        ve1 = cross_part("ve1", [P, 2])
        x1 = cross_part("x1", [P, 2, D])
        x1b = cross_part("x1b", [P, TILES, D])
        x1t = cross_part("x1t", [P, 2, P])
        qt = cross_part("qt", [P, 2, P])
        g_sb = cross_part("g_sb", [P, 2, BT, GW])
        t_sb = cross_part("t_sb", [P, 2, BT, D])
        m_sb = cross_part("m_sb", [P, 2, BT, 32])
        vs_sb = cross_part("vs_sb", [P, 2, BT])
        rv_sb = cross_part("rv_sb", [P, 2, P])
        ct_sb = cross_part("ct_sb", [P, 2, P])
        y_sb = cross_part("y_sb", [P, 2, D])
        stn = cross_part("stn", [P, 2, 6])
        mvn = cross_part("mvn", [P, 2, 2])
        rsn = cross_part("rsn", [P, 2])
        ven = cross_part("ven", [P, 2])
        yn = cross_part("yn", [P, 2, D])
        fin = cross_part("fin", [P, 2, D])
        fin2 = cross_part("fin2", [P, 2, D])
        st2 = cross_part("st2", [P, 2, 6])
        mv2 = cross_part("mv2", [P, 2, 2])
        rs2 = cross_part("rs2", [P, 2])
        ve2 = cross_part("ve2", [P, 2])
        xn = cross_part("xn", [P, 2, D])
        xnt = cross_part("xnt", [P, 2, P])
        v_st = cross_part("v_st", [P, 2, D])
        qv = sb("qv", [P, 2, NB])
        pos_st = sb("pos_st", [P, 2, HEADS * S])
        pos_sb = attend_part("pos_sb", [P, 2, GT, HEADS * S])
        v_rep = attend_part("v_rep", [P, 2, GT * BT, D])
        qu = attend_part("qu", [P, 2, P])
        sc = attend_part("sc", [P, 2, HEADS * S])
        mx = attend_part("mx", [P, 2, HEADS])
        z_sb = attend_part("z_sb", [P, 2, HEADS * S])
        e_sb = attend_part("e_sb", [P, 2, HEADS * S])
        et = attend_part("et", [P, 2, HG, P])
        rden = attend_part("rden", [P, 2, HG, HG])
        cn = attend_part("cn", [P, 2, D])
        cnt = attend_part("cnt", [P, 2, P])
        st3 = feed_part("st3", [P, 2, 6])
        mv3 = feed_part("mv3", [P, 2, 2])
        ve3 = feed_part("ve3", [P, 2])
        rs3 = feed_part("rs3", [P, 2])
        x3 = feed_part("x3", [P, 2, D])
        x3t = feed_part("x3t", [P, 2, P])
        lg = feed_part("lg", [P, 2, EXPERTS])
        m8 = feed_part("m8", [P, 2, 8])
        dz = feed_part("dz", [P, 2])
        th = feed_part("th", [P, 2])
        side = feed_part("side", [P, 2, EXPERTS])
        share = feed_part("share", [P, 2, EXPERTS])
        cmp_gt = feed_part("cmp_gt", [P, 2, EXPERTS, EXPERTS])
        cmp_eq = feed_part("cmp_eq", [P, 2, EXPERTS, EXPERTS])
        rank = feed_part("rank", [P, 2, EXPERTS])
        gates = feed_part("gates", [P, 2, EXPERTS])
        sg = feed_part("sg", [P, 2, FF])
        sgg = feed_part("sgg", [P, 2, FR])
        hh = feed_part("hh", [P, 2, FF])
        ht = feed_part("ht", [P, 2, FF])

        bank = [ctx.enter_context(nc.psum_tensor(f"bank{n}", [P, 512], f32)) for n in range(8)]

        weights_in, x_in, mask_in = sem("weights_in"), sem("x_in"), sem("mask_in")
        ctx_in = [sem("ctx_in0"), sem("ctx_in1")]
        half_set, ones_set, last_ones_set, zeros_set = sem("half_set"), sem("ones_set"), sem("last_ones_set"), sem("zeros_set")
        cols_set, flag_set, ftile_set, poison_sum, poison_set = (
            sem("cols_set"), sem("flag_set"), sem("ftile_set"), sem("poison_sum"), sem("poison_set"))
        pos_keys, pos_blk_set, bk_set = sem("pos_keys"), sem("pos_blk_set"), sem("bk_set")
        st1_done, mv1_done, ve1_done, rs1_done, x1_done = (sem(n) for n in ("st1_done", "mv1_done", "ve1_done", "rs1_done", "x1_done"))
        x1b_done = sem("x1b_done")
        xt_ps, xt_done, qt_ps, qt_done, r_ps, g_ps, g_done = (
            sem(n) for n in ("xt_ps", "xt_done", "qt_ps", "qt_done", "r_ps", "g_ps", "g_done"))
        t_ps, t_done, vs_ps, vs_done, rv_done, m_ps, m_done = (
            sem(n) for n in ("t_ps", "t_done", "vs_ps", "vs_done", "rv_done", "m_ps", "m_done"))
        c_ps, ct_done, y_ps, y_done = (sem(n) for n in ("c_ps", "ct_done", "y_ps", "y_done"))
        stn_done, mvn_done, ven_done, rsn_done, yn_done, fin_mul, fin_add, x_new = (
            sem(n) for n in ("stn_done", "mvn_done", "ven_done", "rsn_done", "yn_done", "fin_mul", "fin_add", "x_new"))
        st2_done, mv2_done, ve2_done, rs2_done, xn_done = (sem(n) for n in ("st2_done", "mv2_done", "ve2_done", "rs2_done", "xn_done"))
        xnt_ps, xnt_done, qk_ps, q_done, k_done, v_ps, v_done = (
            sem(n) for n in ("xnt_ps", "xnt_done", "qk_ps", "q_done", "k_done", "v_ps", "v_done"))
        v_stored = [sem("v_stored0"), sem("v_stored1")]
        qv_done, p_ps, p_done = sem("qv_done"), sem("p_ps"), sem("p_done")
        pos_stored = [sem("pos_stored0"), sem("pos_stored1")]
        pos_in = [sem("pos_in0"), sem("pos_in1")]
        vrep_in = [sem("vrep_in0"), sem("vrep_in1")]
        kblk_in = [sem("kblk_in0"), sem("kblk_in1")]
        vblk_done, xb_done, qu_done, s_ps, sc_done, mx_done, z_done, e_done = (
            sem(n) for n in ("vblk_done", "xb_done", "qu_done", "s_ps", "sc_done", "mx_done", "z_done", "e_done"))
        et_ps, et_done, o_ps, rden_done, cn_done, cnt_ps, cnt_done, a_ps, x_att = (
            sem(n) for n in ("et_ps", "et_done", "o_ps", "rden_done", "cn_done", "cnt_ps", "cnt_done", "a_ps", "x_att"))
        st3_done, mv3_done, ve3_done, rs3_done, x3_done = (sem(n) for n in ("st3_done", "mv3_done", "ve3_done", "rs3_done", "x3_done"))
        x3t_ps, x3t_done, ab_ps, ffb_ps, sg_done = (sem(n) for n in ("x3t_ps", "x3t_done", "ab_ps", "ffb_ps", "sg_done"))
        lg_ps, lg_done, m8_done, dz_done, th_done, side_done, share_done, gt_done, eq_done, eql_done, cmp_done, rank_done, gates_done = (
            sem(n) for n in ("lg_ps", "lg_done", "m8_done", "dz_done", "th_done", "side_done", "share_done", "gt_done", "eq_done",
                             "eql_done", "cmp_done", "rank_done", "gates_done"))
        sgg_done, h_done, ht_ps, ht_done, f_ps, x_out = (
            sem(n) for n in ("sgg_done", "h_done", "ht_ps", "ht_done", "f_ps", "x_out"))
        out_stored = [sem("out_stored0"), sem("out_stored1")]

        x_tok = x.rearrange("(t b) s d -> (b s) t d", b=BT)
        out_tok = out.rearrange("(t b) s d -> t (b s) d", b=BT)

        def at(buf, t):
            return buf[:, bass.ds(t, 1), :].rearrange("p o n -> p (o n)")

        def dram_at(ap, t):
            return ap[bass.ds(t, 1)].rearrange("o p n -> (o p) n")

        def pipeline(eng, step, depth, unroll=2):
            peel = -(-depth // unroll) * unroll
            for i in range(peel):
                step(i, i % unroll, lambda k, i=i: i >= k)
            with eng.Fori(0, (TILES - peel) // unroll) as turn:
                for n in range(unroll):
                    step(unroll * turn + (peel + n), n, lambda k: True)
            for i in range(TILES, TILES + depth):
                step(i, i % unroll, lambda k, i=i: i - k < TILES)

        def rounds(eng, body, total):
            body(0, 0, True)
            body(1, 1, True)
            with eng.Fori(0, total // 2 - 1) as pair:
                for slot in range(2):
                    body(2 * pair + (2 + slot), slot, False)

        def loads_in(t, slot, n):
            return t * (8 * n) + (16 * n - 8 * n * slot)

        def group_in(t, m, n):
            return (t - m) * (2 * n) + 16 * n

        def cap(count):
            return min(count, TILES) if isinstance(count, int) else count

        def is_step(i, n):
            return isinstance(i, int) and i == n

        block = ctx.enter_context(nc.Block())

        @block.sync
        def _(sp):
            sp.dma_start(x_all[:], x_tok).then_inc(x_in, 16)
            sp.dma_start(w_sb[:], weights).then_inc(weights_in, 16)
            sp.dma_start(row_sb[:], rows.partition_broadcast(P)).then_inc(weights_in, 16)

            def load_context(i, slot, on):
                if on(0):
                    if on(2):
                        sp.wait_ge(g_ps, 2 * i - 2)
                    sp.dma_start(c_sb[:, slot, :, :, 0:D], ctx_main[bass.ds(i, 1)].rearrange("o p b c d -> (o p) b c d")).then_inc(ctx_in[slot], 16)
                    sp.dma_start(cl_sb[:, slot, :, 0:D], ctx_last[bass.ds(i, 1)]).then_inc(ctx_in[slot], 16)
                if is_step(i, 1):
                    sp.dma_start(mask_sb[:], mask).then_inc(mask_in, 16)
                if on(8):
                    sp.wait_ge(v_done, i - 7)
                    sp.dma_start(dram_at(v_scratch, i - 8), v_st[:, slot, :]).then_inc(v_stored[slot], 16)

            sp.wait_ge(ones_set, 1)
            sp.wait_ge(last_ones_set, 1)
            pipeline(sp, load_context, 8)

            pos_tok = pos_scratch.rearrange("(t b) i n -> t (b i) n", b=BT)
            v_tok = v_scratch.rearrange("t (b j) d -> j (t b) d", b=BT)

            def store_position(i, slot):
                sp.wait_ge(p_done, i + 3)
                sp.dma_start(pos_scratch[:, bass.ds(i, 1), :].rearrange("b o n -> b (o n)"), pos_st[:, slot, :]).then_inc(pos_stored[slot], 16)

            def load_keys(g, slot, h):
                sp.dma_start(k_blk[HD * h:HD * h + HD, slot, h, :],
                             k_all[HD * h:HD * h + HD, bass.ds(g * (GT * P), GT * P)]).then_inc(kblk_in[slot], 16)

            def load_values(g, slot):
                for h in range(HG):
                    sp.dma_start(v_rep[S * h:S * h + S, slot, :, :], v_tok[:, bass.ds(g * (GT * BT), GT * BT), :]).then_inc(vrep_in[slot], 16)

            with sp.Fori(0, S // 4) as pair:
                for slot in range(2):
                    store_position(2 * pair + slot, slot)
            sp.wait_ge(k_done, TILES)
            sp.wait_ge(zeros_set, 1)
            for i in range(S // 2, S):
                store_position(i, i % 2)
                load_keys(0, 0, i - S // 2)
            for s in range(2):
                sp.wait_ge(v_stored[s], 16 * TILES // 2)
            load_values(0, 0)
            for s in range(2):
                sp.wait_ge(pos_stored[s], 16 * S // 2)
            sp.wait_ge(zeros_set, 2)

            def load_group(g, slot, first):
                if not first:
                    sp.wait_ge(sc_done, GT * g - GT)
                sp.dma_start(pos_sb[:, slot, :, :], pos_tok[bass.ds(g * GT, GT)].rearrange("t p n -> p t n")).then_inc(pos_in[slot], 16)
                if is_step(g, 0):
                    return
                if not first:
                    sp.wait_ge(s_ps, GT * g - GT)
                for h in range(HEADS):
                    load_keys(g, slot, h)
                if not first:
                    sp.wait_ge(vblk_done, GT * g - GT)
                load_values(g, slot)

            rounds(sp, load_group, TILES // GT)

            with sp.Fori(0, TILES // 2) as pair:
                for slot in range(2):
                    t = 2 * pair + slot
                    sp.wait_ge(x_out, t + 1)
                    sp.dma_start(dram_at(out_tok, t), at(x_all, t)).then_inc(out_stored[slot], 16)
            for s in range(2):
                sp.wait_ge(out_stored[s], 16 * TILES // 2)

        @block.gpsimd
        def _(pool):
            pool.memset(half[:], -0.5).then_inc(half_set, 1)
            pool.memset(c_sb[:, :, :, :, D:GW], 1.0).then_inc(ones_set, 1)
            pool.memset(cl_sb[:, :, :, D:GW], 1.0).then_inc(last_ones_set, 1)
            pool.wait_ge(weights_in, 32)
            pool.wait_ge(x_in, 16)
            pool.wait_ge(half_set, 1)

            def cross(i, slot, on):
                other = (slot + 1) % 2
                if on(0):
                    pool.wait_ge(ve1_done, i + 1)
                    pool.tensor_tensor(rs1[:, slot:slot + 1], ve1[:, slot:slot + 1], half[:], ALU.pow).then_inc(rs1_done, 1)
                if on(1):
                    pool.wait_ge(x1_done, i)
                    pool.tensor_tensor(at(x1b, i - 1), x1[:, other, :], ROW("xbo"), ALU.add).then_inc(x1b_done, 1)
                if on(4):
                    pool.wait_ge(ven_done, i - 3)
                    pool.tensor_tensor(rsn[:, slot:slot + 1], ven[:, slot:slot + 1], half[:], ALU.pow).then_inc(rsn_done, 1)
                if on(6):
                    pool.wait_ge(ve2_done, i - 5)
                    pool.tensor_tensor(rs2[:, slot:slot + 1], ve2[:, slot:slot + 1], half[:], ALU.pow).then_inc(rs2_done, 1)
                if on(5):
                    pool.wait_ge(yn_done, i - 4)
                    pool.tensor_tensor(fin[:, other, :], yn[:, other, :], ROW("ln_g"), ALU.mult).then_inc(fin_mul, 1)
                    pool.wait_ge(fin_mul, i - 4)
                    pool.tensor_tensor(fin2[:, other, :], fin[:, other, :], ROW("ln_b"), ALU.add).then_inc(fin_add, 1)
                    pool.wait_ge(fin_add, i - 4)
                    pool.tensor_tensor(at(x_all, i - 5), at(x_all, i - 5), fin2[:, other, :], ALU.add).then_inc(x_new, 1)

            pipeline(pool, cross, 6)

            for s in range(2):
                pool.memset(k_blk[:, s], 0.0).then_inc(zeros_set, 1)
            pool.wait_ge(ct_done, TILES)

            for s in range(2):
                pool.tensor_copy(v_blk[:, s, :, :, 32:OW].rearrange("p b g o -> p (b g) o"),
                                 W("ones4").unsqueeze(1).broadcast_to([P, BT * HG, 4])).then_inc(zeros_set, 1)

            pool.wait_ge(x_new, TILES)
            pool.wait_ge(xn_done, TILES)

            def spread(t, n, on):
                slot, group, r = n % 2, n // GT, n % GT
                if r == 0:
                    pool.wait_ge(vrep_in[group], group_in(t, n, HG))
                if on(2):
                    pool.wait_ge(o_ps, t - 1)
                pool.tensor_tensor(v_blk[:, slot, :, :, 0:32], v_rep[:, group, BT * r:BT * r + BT, :].rearrange("p b (g n) -> p b g n", g=HG),
                                   W("vmask").unsqueeze(1).unsqueeze(1).broadcast_to([P, BT, HG, 32]), ALU.mult).then_inc(vblk_done, 1)
                pool.tensor_tensor(at(x_all, t), at(x_all, t), ROW("abo"), ALU.add).then_inc(xb_done, 1)

            for t in range(2 * GT):
                spread(t, t, lambda k, t=t: t >= k)
            with pool.Fori(0, TILES // (2 * GT) - 1) as turn:
                for n in range(2 * GT):
                    spread(2 * GT * turn + (2 * GT + n), n, lambda k: True)

            def gate(i, slot, on):
                if on(0):
                    pool.wait_ge(ve3_done, i + 1)
                    pool.tensor_tensor(rs3[:, slot:slot + 1], ve3[:, slot:slot + 1], half[:], ALU.pow).then_inc(rs3_done, 1)
                if on(2):
                    pool.wait_ge(sg_done, i - 1)
                    pool.wait_ge(gates_done, i - 1)
                    pool.tensor_tensor(sgg[:, slot, :].rearrange("p (e n) -> p e n", e=EXPERTS), sg[:, slot, 0:FR].rearrange("p (e n) -> p e n", e=EXPERTS),
                                       gates[:, slot, :].unsqueeze(2).broadcast_to([P, EXPERTS, HID]), ALU.mult).then_inc(sgg_done, 1)

            pipeline(pool, gate, 2)

        @block.scalar
        def _(act):
            act.wait_ge(weights_in, 32)
            act.wait_ge(cols_set, 4)

            def cross(i, slot, on):
                if on(0):
                    act.wait_ge(xt_ps, i + 1)
                    act.activation(x1t[:, slot, :], bank[0][:, 0:P], ACT.Copy).then_inc(xt_done, 1)
                    if on(2):
                        act.wait_ge(vs_ps, i - 1)
                    act.wait_ge(g_ps, 2 * i + 1)
                    act.activation(g_sb[:, slot, 0:2, :], bank[2][:, 0:2 * GW].rearrange("p (b n) -> p b n", b=2), ACT.Copy).then_inc(g_done, 1)
                    if on(2):
                        act.wait_ge(c_ps, i - 1)
                    act.wait_ge(qt_ps, i + 1)
                    act.activation(qt[:, slot, :], bank[0][:, P:2 * P], ACT.Identity, bias=xbq_s, scale=1.0 / DK).then_inc(qt_done, 1)
                if on(5):
                    s = (slot + 1) % 2
                    if on(7):
                        act.wait_ge(v_ps, i - 6)
                        act.wait_ge(qk_ps, i - 6)
                    act.wait_ge(xnt_ps, i - 4)
                    act.activation(xnt[:, s, :], bank[7][:, 0:P], ACT.Identity, bias=W("beta"), scale=W("gamma")).then_inc(xnt_done, 1)
                if on(0):
                    act.wait_ge(g_ps, 2 * i + 2)
                    act.activation(g_sb[:, slot, 2:4, :], bank[3][:, 0:2 * GW].rearrange("p (b n) -> p b n", b=2), ACT.Copy).then_inc(g_done, 1)
                if on(5):
                    act.wait_ge(qk_ps, i - 4)
                    act.activation(q_all[:, bass.ds((i - 5) * BT, BT), :].rearrange("p b s -> p (b s)"), bank[7][:, P:2 * P], ACT.Copy).then_inc(q_done, 1)
                    act.activation(k_all[:, bass.ds((i - 5) * P, P)], bank[7][:, 2 * P:3 * P], ACT.Identity, bias=W("abk")).then_inc(k_done, 1)

            pipeline(act, cross, 7)

            act.wait_ge(q_done, TILES)
            with act.Fori(0, S // 2) as pair:
                for slot in range(2):
                    i = 2 * pair + slot
                    act.wait_ge(p_ps, i + 1)
                    act.activation(qv[:, slot, :], q_all[:, :, bass.ds(i, 1)].rearrange("p b o -> p (b o)"), ACT.Identity, bias=qv_b).then_inc(qv_done, 1)

            def attend(i, n, on):
                slot = n % 2
                if on(0):
                    if on(2):
                        act.wait_ge(s_ps, i - 1)
                    act.activation(qu[:, slot, :], q_all[:, bass.ds(i * BT, BT), :].rearrange("p b s -> p (b s)"), ACT.Identity, bias=qu_b).then_inc(qu_done, 1)
                if on(2):
                    act.wait_ge(z_done, i - 1)
                    if on(4):
                        act.wait_ge(et_ps, i - 3)
                    act.activation(e_sb[:, slot, :], z_sb[:, slot, :], ACT.Exp, scale=1.0 / math.sqrt(HD)).then_inc(e_done, 1)
                    act.wait_ge(et_ps, i - 1)
                    if on(4):
                        act.wait_ge(o_ps, i - 3)
                    act.activation(et[:, slot, :, :].rearrange("p g n -> p (g n)"), bank[2 + slot][:, :], ACT.Copy).then_inc(et_done, 1)
                if on(3):
                    s = (slot + 1) % 2
                    act.wait_ge(cnt_ps, i - 2)
                    if on(5):
                        act.wait_ge(a_ps, i - 4)
                    act.activation(cnt[:, s, :], bank[5][:, 0:P], ACT.Copy).then_inc(cnt_done, 1)

            pipeline(act, attend, 5)

            def feed(i, slot, on):
                if on(0):
                    act.wait_ge(x3t_ps, i + 1)
                    if on(2):
                        act.wait_ge(ffb_ps, i - 1)
                    act.activation(x3t[:, slot, :], bank[6][:, 0:P], ACT.Copy).then_inc(x3t_done, 1)
                if on(2):
                    act.wait_ge(ht_ps, i - 1)
                    if on(4):
                        act.wait_ge(f_ps, i - 3)
                    act.activation(ht[:, slot, 512:FF], bank[2 + 2 * slot][:, 2 * FS:3 * FS], ACT.Copy)
                    act.activation(ht[:, slot, 0:512], bank[3][:, :], ACT.Copy).then_inc(ht_done, 1)
                if on(0):
                    act.wait_ge(dz_done, i + 1)
                    act.activation(th[:, slot:slot + 1], dz[:, slot:slot + 1], ACT.Tanh, scale=0.5).then_inc(th_done, 1)
                    if on(2):
                        act.wait_ge(h_done, i - 1)
                        act.wait_ge(sgg_done, i - 1)
                    act.wait_ge(ab_ps, i + 1)
                    act.activation(sg[:, slot, 0:FR], bank[0][:, :], ACT.Silu)
                    act.wait_ge(ffb_ps, i + 1)
                    act.activation(sg[:, slot, FR:FF], bank[2 + 2 * slot][:, 0:FS], ACT.Silu).then_inc(sg_done, 1)

            pipeline(act, feed, 4)

        @block.vector
        def _(dve):
            dve.wait_ge(weights_in, 32)
            dve.tensor_scalar(xbq_s, W("xbq"), 1.0 / DK, None, ALU.mult).then_inc(cols_set, 1)
            dve.tensor_scalar(xbv_n, W("xbv"), float(S2), None, ALU.mult).then_inc(cols_set, 1)
            dve.tensor_tensor(qu_b, W("abq"), W("u"), ALU.add).then_inc(cols_set, 1)
            dve.tensor_tensor(qv_b, W("abq"), W("v"), ALU.add).then_inc(cols_set, 1)
            dve.tensor_scalar(bk_heads[:], W("blk128"), W("xbk"), None, ALU.mult).then_inc(bk_set, 1)
            dve.wait_ge(pos_keys, 1)
            dve.tensor_tensor(pos_blk[:], bank[1][:, 0:POS].unsqueeze(1).broadcast_to([P, HEADS, POS]),
                              W("head16").unsqueeze(2).broadcast_to([P, HEADS, POS]), ALU.mult).then_inc(pos_blk_set, 1)
            dve.wait_ge(x_in, 16)
            dve.wait_ge(cols_set, 4)

            def moments(slot, src, stat, mv, ve, st_sem, mv_sem, ve_sem, count, scale, eps):
                dve.bn_stats(stat[:, slot, :], src).then_inc(st_sem, 1)
                dve.wait_ge(st_sem, count)
                dve.nop(nofuse=True)
                dve.bn_aggr(mv[:, slot, :], stat[:, slot, :]).then_inc(mv_sem, 1)
                dve.wait_ge(mv_sem, count)
                dve.tensor_scalar(ve[:, slot:slot + 1], mv[:, slot, 1:2], scale, eps, ALU.mult, ALU.add).then_inc(ve_sem, 1)

            def mask_flags():
                dve.wait_ge(mask_in, 16)
                dve.tensor_reduce(flag[:, 0:1], mask_sb[:].bitcast(mybir.dt.int32), AX, ALU.max).then_inc(flag_set, 1)
                dve.wait_ge(flag_set, 1)
                dve.tensor_scalar(flag[:, 1:2], flag[:, 0:1], 0.0, None, ALU.is_gt).then_inc(flag_set, 1)
                dve.wait_ge(flag_set, 2)
                dve.tensor_scalar(flag_tile[:], W("batch_tile"), flag[:, 1:2], None, ALU.mult).then_inc(ftile_set, 1)

            def mask_poison():
                dve.wait_ge(poison_sum, 1)
                dve.tensor_scalar(poison[:], bank[6][:, 0:TILES], -3.0e38, 3.0e38, ALU.mult, ALU.mult).then_inc(poison_set, 1)
                dve.wait_ge(poison_set, 1)

            def cross(i, slot, on):
                other = (slot + 1) % 2
                if on(1):
                    if on(3):
                        dve.wait_ge(xt_ps, i - 2)
                        dve.wait_ge(x1b_done, i - 2)
                    dve.wait_ge(rs1_done, i)
                    dve.tensor_scalar(x1[:, other, :], at(x_all, i - 1), mv1[:, other, 0:1], rs1[:, other:other + 1], ALU.subtract, ALU.mult).then_inc(x1_done, 1)
                if on(6):
                    dve.wait_ge(x_new, i - 5)
                    moments(slot, at(x_all, i - 6), st2, mv2, ve2, st2_done, mv2_done, ve2_done, i - 5, 1.0 + EPS, EPS * EPS)
                if on(0):
                    moments(slot, at(x_all, i), st1, mv1, ve1, st1_done, mv1_done, ve1_done, i + 1, 1.0, EPS)
                if is_step(i, 4):
                    mask_poison()
                if on(4):
                    dve.wait_ge(y_ps, i - 3)
                    dve.wait_ge(x1b_done, i - 3)
                    dve.scalar_tensor_tensor(y_sb[:, slot, :], bank[6][:, 0:D], poison[:, bass.ds(i - 4, 1)], at(x1b, i - 4),
                                             ALU.add, ALU.add).then_inc(y_done, 1)
                    dve.wait_ge(y_done, i - 3)
                    moments(slot, y_sb[:, slot, :], stn, mvn, ven, stn_done, mvn_done, ven_done, i - 3, 1.0, EPS)
                if on(3):
                    dve.wait_ge(m_ps, i - 2)
                    dve.tensor_tensor(m_sb[:, other, :, :], bank[5][:, 0:BT * 32].rearrange("p (b n) -> p b n", b=BT),
                                      W("blk32").unsqueeze(1).broadcast_to([P, BT, 32]), ALU.mult).then_inc(m_done, 1)
                if on(6):
                    if on(8):
                        dve.wait_ge(xnt_ps, i - 7)
                    dve.wait_ge(rs2_done, i - 5)
                    dve.tensor_scalar(xn[:, slot, :], at(x_all, i - 6), mv2[:, slot, 0:1], rs2[:, slot:slot + 1], ALU.subtract, ALU.mult).then_inc(xn_done, 1)
                if on(7):
                    dve.wait_ge(v_ps, i - 6)
                    if on(9):
                        dve.wait_ge(v_stored[other], loads_in(i - 9, other, 1))
                    dve.tensor_tensor(v_st[:, other, :], bank[6][:, P:2 * P], ROW("abv"), ALU.add).then_inc(v_done, 1)
                if on(2):
                    dve.wait_ge(t_ps, i - 1)
                    for b in range(BT):
                        dve.scalar_tensor_tensor(t_sb[:, slot, b, :], ROW("xbv"), g_sb[:, slot, b, D:GW],
                                                 bank[4][:, b * D:(b + 1) * D], ALU.mult, ALU.add).then_inc(t_done, 1)
                if on(3):
                    dve.wait_ge(c_ps, i - 2)
                    dve.wait_ge(rv_done, i - 2)
                    dve.tensor_tensor(ct_sb[:, other, :], bank[5][:, P:2 * P], rv_sb[:, other, :], ALU.add).then_inc(ct_done, 1)
                if on(2):
                    dve.wait_ge(vs_ps, i - 1)
                    dve.tensor_scalar(vs_sb[:, slot, :], bank[1][:, P:P + BT], xbv_n, None, ALU.add).then_inc(vs_done, 1)
                if on(4):
                    if on(6):
                        dve.wait_ge(fin_mul, i - 5)
                    dve.wait_ge(rsn_done, i - 3)
                    dve.tensor_scalar(yn[:, slot, :], y_sb[:, slot, :], mvn[:, slot, 0:1], rsn[:, slot:slot + 1], ALU.subtract, ALU.mult).then_inc(yn_done, 1)
                if on(2):
                    dve.wait_ge(vs_done, i - 1)
                    dve.wait_ge(r_ps, i - 1)
                    dve.tensor_tensor(rv_sb[:, slot, :].rearrange("p (b s) -> p b s", b=BT), bank[1][:, 0:P].rearrange("p (b s) -> p b s", b=BT),
                                      vs_sb[:, slot, :].unsqueeze(2).broadcast_to([P, BT, S]), ALU.mult).then_inc(rv_done, 1)
                if is_step(i, 2):
                    mask_flags()

            pipeline(dve, cross, 9)

            dve.sem_inc(p_done, 2)

            def keep_positions(i, slot, first):
                dve.wait_ge(p_ps, i + 3)
                if not first:
                    dve.wait_ge(pos_stored[slot], loads_in(i - 2, slot, 1))
                dve.tensor_copy(pos_st[:, slot, :], bank[slot][:, :]).then_inc(p_done, 1)

            rounds(dve, keep_positions, S)

            def heads(ap):
                return ap.rearrange("p (h j) -> p h j", h=HEADS)

            def attend(i, n, on):
                slot, other = n % 2, (n + 1) % 2
                if on(0):
                    dve.wait_ge(s_ps, i + 1)
                    if n % GT == 0:
                        dve.wait_ge(pos_in[n // GT], group_in(i, n, 1))
                    dve.tensor_tensor(sc[:, slot, :], bank[slot][:, :], pos_sb[:, n // GT, n % GT, :], ALU.add).then_inc(sc_done, 1)
                if on(2):
                    dve.wait_ge(o_ps, i - 1)
                    dve.reciprocal(rden[:, slot, :, :], bank[4][:, 0:HG * OW].rearrange("p (g n) -> p g n", g=HG)[:, :, 32:OW]).then_inc(rden_done, 1)
                if on(0):
                    dve.wait_ge(sc_done, i + 1)
                    dve.tensor_reduce(mx[:, slot, :], heads(sc[:, slot, :]), AX, ALU.max).then_inc(mx_done, 1)
                if on(2):
                    dve.wait_ge(rden_done, i - 1)
                    if on(4):
                        dve.wait_ge(cnt_ps, i - 3)
                    dve.tensor_tensor(cn[:, slot, :].rearrange("p (g h n) -> p g h n", g=HG, h=HG),
                                      bank[4][:, 0:HG * OW].rearrange("p (g n) -> p g n", g=HG)[:, :, 0:32].rearrange("p g (h n) -> p g h n", h=HG),
                                      rden[:, slot, :, :].unsqueeze(3).broadcast_to([P, HG, HG, HD]), ALU.mult).then_inc(cn_done, 1)
                if on(0):
                    dve.wait_ge(mx_done, i + 1)
                    if on(2):
                        dve.wait_ge(e_done, i - 1)
                    dve.tensor_tensor(heads(z_sb[:, slot, :]), heads(sc[:, slot, :]),
                                      mx[:, slot, :].unsqueeze(2).broadcast_to([P, HEADS, S]), ALU.subtract).then_inc(z_done, 1)
                if on(3):
                    dve.wait_ge(a_ps, i - 2)
                    dve.wait_ge(xb_done, i - 2)
                    dve.tensor_tensor(at(x_all, i - 3), bank[6][:, 0:D], at(x_all, i - 3), ALU.add).then_inc(x_att, 1)

            pipeline(dve, attend, 4, 2 * GT)

            def feed(i, slot, on):
                other = (slot + 1) % 2
                L = lg[:, slot, :]
                mine = L.unsqueeze(2).broadcast_to([P, EXPERTS, EXPERTS])
                theirs = L.unsqueeze(1).broadcast_to([P, EXPERTS, EXPERTS])
                if on(5):
                    dve.wait_ge(f_ps, i - 4)
                    dve.tensor_tensor(at(x_all, i - 5), bank[5][:, 0:D], at(x_all, i - 5), ALU.add).then_inc(x_out, 1)
                if on(1):
                    if on(3):
                        dve.wait_ge(x3t_ps, i - 2)
                    dve.wait_ge(rs3_done, i)
                    dve.tensor_scalar(x3[:, other, :], at(x_all, i - 1), mv3[:, other, 0:1], rs3[:, other:other + 1], ALU.subtract, ALU.mult).then_inc(x3_done, 1)
                if on(2):
                    dve.wait_ge(lg_ps, i - 1)
                    dve.tensor_tensor(L, bank[6][:, P:P + EXPERTS], ROW("rb"), ALU.add).then_inc(lg_done, 1)
                if on(3):
                    if on(5):
                        dve.wait_ge(ht_ps, i - 4)
                    dve.wait_ge(sg_done, i - 2)
                    dve.tensor_tensor(hh[:, other, FR:FF], bank[2 + 2 * other][:, FS:2 * FS], sg[:, other, FR:FF], ALU.mult)
                if on(2):
                    dve.wait_ge(lg_done, i - 1)
                    dve.nop(nofuse=True)
                    dve.max(m8[:, slot, :], L).then_inc(m8_done, 1)
                    dve.tensor_tensor(cmp_eq[:, slot], theirs, mine, ALU.is_equal).then_inc(eq_done, 1)
                    dve.wait_ge(m8_done, i - 1)
                    dve.tensor_tensor(dz[:, slot:slot + 1], m8[:, slot, 0:1], m8[:, slot, 1:2], ALU.subtract).then_inc(dz_done, 1)
                    dve.tensor_tensor(cmp_gt[:, slot], theirs, mine, ALU.is_gt).then_inc(gt_done, 1)
                    dve.wait_ge(eq_done, i - 1)
                    dve.tensor_tensor(cmp_eq[:, slot], cmp_eq[:, slot], W("lower").rearrange("p (a b) -> p a b", a=EXPERTS), ALU.mult).then_inc(eql_done, 1)
                if on(3):
                    dve.wait_ge(sgg_done, i - 2)
                    dve.tensor_tensor(hh[:, other, 0:FR], bank[1 + 6 * other][:, :], sgg[:, other, :], ALU.mult).then_inc(h_done, 1)
                if on(2):
                    dve.wait_ge(eql_done, i - 1)
                    dve.wait_ge(gt_done, i - 1)
                    dve.tensor_tensor(cmp_gt[:, slot], cmp_gt[:, slot], cmp_eq[:, slot], ALU.add).then_inc(cmp_done, 1)
                if on(0):
                    if is_step(i, 0):
                        dve.wait_ge(x_att, TILES)
                    dve.bn_stats(st3[:, slot, :], at(x_all, i)).then_inc(st3_done, 1)
                if on(2):
                    dve.wait_ge(cmp_done, i - 1)
                    dve.tensor_reduce(rank[:, slot, :], cmp_gt[:, slot], AX, ALU.add).then_inc(rank_done, 1)
                if on(0):
                    dve.wait_ge(st3_done, i + 1)
                    dve.nop(nofuse=True)
                    dve.bn_aggr(mv3[:, slot, :], st3[:, slot, :]).then_inc(mv3_done, 1)
                if on(2):
                    dve.wait_ge(rank_done, i - 1)
                    dve.tensor_scalar(side[:, slot, :], rank[:, slot, :], -1.0, 0.5, ALU.mult, ALU.add).then_inc(side_done, 1)
                if on(0):
                    if on(2):
                        dve.wait_ge(rs3_done, i - 1)
                    dve.wait_ge(mv3_done, i + 1)
                    dve.tensor_scalar(ve3[:, slot:slot + 1], mv3[:, slot, 1:2], 1.0, EPS, ALU.mult, ALU.add).then_inc(ve3_done, 1)
                if on(2):
                    dve.wait_ge(side_done, i - 1)
                    dve.wait_ge(th_done, i - 1)
                    dve.tensor_scalar(share[:, slot, :], side[:, slot, :], th[:, slot:slot + 1], 0.5, ALU.mult, ALU.add).then_inc(share_done, 1)
                    dve.wait_ge(share_done, i - 1)
                    if on(4):
                        dve.wait_ge(sgg_done, i - 3)
                    dve.scalar_tensor_tensor(gates[:, slot, :], rank[:, slot, :], 2.0, share[:, slot, :], ALU.is_lt, ALU.mult).then_inc(gates_done, 1)

            pipeline(dve, feed, 5)

        @block.tensor
        def _(pe):
            pe.wait_ge(weights_in, 32)
            mm = nc.tensor.matmul
            ident = W("ident")
            mm(bank[1][:, 0:POS], W("awp"), W("pe"), start=True, stop=True).then_inc(pos_keys, 1)
            pe.wait_ge(pos_blk_set, 1)
            pe.wait_ge(bk_set, 1)

            def cross(j, slot, on):
                other = (slot + 1) % 2

                def gram(half):
                    g = bank[2 + half]
                    for n in range(2):
                        b = 2 * half + n
                        o = g[:, n * GW:(n + 1) * GW]
                        mm(o, c_sb[:, slot, b, 0, 0:D], c_sb[:, slot, b, 0, :], start=True, stop=False)
                        mm(o, c_sb[:, slot, b, 1, 0:D], c_sb[:, slot, b, 1, :], start=False, stop=False)
                        last = mm(o, cl_sb[:, slot, b, 0:D], cl_sb[:, slot, b, :], start=False, stop=True)
                    last.then_inc(g_ps, 1)

                if on(0):
                    pe.wait_ge(x1_done, j + 1)
                    nc.tensor.transpose(bank[0][:, 0:P], x1[:, slot, :], ident).then_inc(xt_ps, 1)
                    pe.wait_ge(ctx_in[slot], loads_in(j, slot, 2))
                    gram(0)
                    pe.wait_ge(xt_done, j + 1)
                    mm(bank[0][:, P:2 * P], W("xwq"), x1t[:, slot, :], start=True, stop=True).then_inc(qt_ps, 1)
                if on(5):
                    if on(6):
                        pe.wait_ge(k_done, j - 5)
                    pe.wait_ge(xn_done, j - 4)
                    nc.tensor.transpose(bank[7][:, 0:P], xn[:, other, :], ident).then_inc(xnt_ps, 1)
                if on(2):
                    if on(6):
                        pe.wait_ge(v_done, j - 5)
                    if is_step(j, 2):
                        pe.wait_ge(ftile_set, 1)
                        mm(bank[6][:, 0:TILES], W("batch_row"), flag_tile[:], start=True, stop=True).then_inc(poison_sum, 1)
                        pe.wait_ge(poison_set, 1)
                    pe.wait_ge(ct_done, j - 1)
                    if on(3):
                        pe.wait_ge(y_done, j - 2)
                    mm(bank[6][:, 0:D], ct_sb[:, slot, :], W("xwo"), start=True, stop=True).then_inc(y_ps, 1)
                if on(0):
                    gram(1)
                    pe.wait_ge(qt_done, j + 1)
                    if on(1):
                        pe.wait_ge(rv_done, j)
                    mm(bank[1][:, 0:P], bk_heads[:], qt[:, slot, :], start=True, stop=True).then_inc(r_ps, 1)
                if on(5):
                    pe.wait_ge(xnt_done, j - 4)
                    mm(bank[7][:, P:2 * P], W("awq"), xnt[:, other, :], start=True, stop=True)
                    mm(bank[7][:, 2 * P:3 * P], W("awk"), xnt[:, other, :], start=True, stop=True).then_inc(qk_ps, 1)
                    pe.wait_ge(y_done, cap(j - 1))
                    if on(6):
                        pe.wait_ge(v_done, j - 5)
                    mm(bank[6][:, P:2 * P], xnt[:, other, :], W("awv"), start=True, stop=True).then_inc(v_ps, 1)
                if on(1):
                    if on(2):
                        pe.wait_ge(ct_done, j - 1)
                    pe.wait_ge(t_done, BT * j)
                    for g in range(HG):
                        last = mm(bank[5][32 * g:32 * g + 32, 0:BT * 32].rearrange("p (b n) -> p b n", b=BT), W("xwk")[:, 32 * g:32 * g + 32],
                                  t_sb[:, other, :, 32 * g:32 * g + 32], start=True, stop=True)
                    last.then_inc(m_ps, 1)
                if on(0):
                    for b in range(BT):
                        if b % 2 == 0:
                            pe.wait_ge(g_done, 2 * j + 1 + b // 2)
                        last = mm(bank[4][:, b * D:(b + 1) * D], g_sb[:, slot, b, 0:D], W("xwv"), start=True, stop=True)
                    last.then_inc(t_ps, 1)
                    mm(bank[1][:, P:P + BT], W("xwv"), g_sb[:, slot, :, D], start=True, stop=True).then_inc(vs_ps, 1)
                if on(1):
                    pe.wait_ge(m_done, j)
                    pe.nop(nofuse=True)
                    for b in range(BT):
                        for g in range(HG):
                            r = slice(32 * g, 32 * g + 32)
                            last = mm(bank[5][r, P + S * b:P + S * b + S], m_sb[r, other, b, :], qt[r, other, S * b:S * b + S], start=True, stop=True)
                    last.then_inc(c_ps, 1)

            pipeline(pe, cross, 5)

            pe.sem_inc(p_ps, 2)
            pe.wait_ge(ct_done, TILES)
            with pe.Fori(0, S // 2) as pair:
                for slot in range(2):
                    i = 2 * pair + slot
                    pe.wait_ge(qv_done, i + 1)
                    pe.wait_ge(p_done, i + 1)
                    pe.nop(nofuse=True)
                    mm(bank[slot][:, :].rearrange("p (h j) -> p h j", h=HEADS), qv[:, slot, :], pos_blk[:, :, bass.ds((S - 1 - slot) - 2 * pair, S)],
                       start=True, stop=True).then_inc(p_ps, 1)

            pe.wait_ge(p_done, S + 2)
            pe.wait_ge(v_done, TILES)

            def attend(j, n, on):
                slot, other = n % 2, (n + 1) % 2
                if on(0):
                    pe.wait_ge(qu_done, j + 1)
                    if n % GT == 0:
                        pe.wait_ge(kblk_in[n // GT], group_in(j, n, HEADS))
                    if on(2):
                        pe.wait_ge(sc_done, j - 1)
                    for b in range(BT):
                        last = mm(bank[slot][S * b:S * b + S, :].rearrange("p (h j) -> p h j", h=HEADS), qu[:, slot, S * b:S * b + S],
                                  k_blk[:, n // GT, :, P * (n % GT) + S * b:P * (n % GT) + S * b + S], start=True, stop=True)
                    last.then_inc(s_ps, 1)
                if on(2):
                    pe.wait_ge(et_done, j - 1)
                    pe.wait_ge(vblk_done, j - 1)
                    if on(3):
                        pe.wait_ge(cn_done, j - 2)
                    for g in range(HG):
                        for b in range(BT):
                            last = mm(bank[4][S * b:S * b + S, g * OW:(g + 1) * OW], et[:, slot, g, S * b:S * b + S],
                                      v_blk[:, slot, b, g, :], start=True, stop=True)
                    last.then_inc(o_ps, 1)
                if on(1):
                    pe.wait_ge(e_done, j)
                    if on(3):
                        pe.wait_ge(et_done, j - 2)
                    for g in range(HG):
                        last = nc.tensor.transpose(bank[2 + other][:, g * P:(g + 1) * P], e_sb[:, other, g * P:(g + 1) * P], ident)
                    last.then_inc(et_ps, 1)
                if on(2):
                    pe.wait_ge(cn_done, j - 1)
                    if on(3):
                        pe.wait_ge(cnt_done, j - 2)
                    nc.tensor.transpose(bank[5][:, 0:P], cn[:, slot, :], ident).then_inc(cnt_ps, 1)
                if on(3):
                    pe.wait_ge(cnt_done, j - 2)
                    if on(4):
                        pe.wait_ge(x_att, j - 3)
                    mm(bank[6][:, 0:D], cnt[:, other, :], W("awo"), start=True, stop=True).then_inc(a_ps, 1)

            pipeline(pe, attend, 3, 2 * GT)

            pe.wait_ge(x_att, TILES)

            def feed(j, slot, on):
                if on(0):
                    pe.wait_ge(x3_done, j + 1)
                    if on(1):
                        pe.wait_ge(lg_done, j)
                    nc.tensor.transpose(bank[6][:, 0:P], x3[:, slot, :], ident).then_inc(x3t_ps, 1)
                if on(2):
                    pe.wait_ge(h_done, j - 1)
                    if on(3):
                        pe.wait_ge(ht_done, j - 2)
                    for c in range(CHUNKS):
                        o = bank[3][:, c * P:(c + 1) * P] if c < 4 else bank[2 + 2 * slot][:, 2 * FS:3 * FS]
                        last = nc.tensor.transpose(o, hh[:, slot, c * P:(c + 1) * P], ident)
                    last.then_inc(ht_ps, 1)
                if on(0):
                    pe.wait_ge(x3t_done, j + 1)
                    mm(bank[6][:, P:P + EXPERTS], x3t[:, slot, :], W("router"), start=True, stop=True).then_inc(lg_ps, 1)
                    if on(1):
                        pe.wait_ge(sg_done, j)
                    mm(bank[0][:, :], x3t[:, slot, :], W("w1")[:, 0:FR], start=True, stop=True).then_inc(ab_ps, 1)
                    mm(bank[1 + 6 * slot][:, :], x3t[:, slot, :], W("w3")[:, 0:FR], start=True, stop=True)
                    if on(2):
                        pe.wait_ge(ht_done, j - 1)
                    mm(bank[2 + 2 * slot][:, 0:FS], x3t[:, slot, :], W("w1")[:, FR:FF], start=True, stop=True)
                    mm(bank[2 + 2 * slot][:, FS:2 * FS], x3t[:, slot, :], W("w3")[:, FR:FF], start=True, stop=True).then_inc(ffb_ps, 1)
                if on(2):
                    pe.wait_ge(ht_done, j - 1)
                    if on(3):
                        pe.wait_ge(x_out, j - 2)
                    for c in range(CHUNKS):
                        last = mm(bank[5][:, 0:D], ht[:, slot, c * P:(c + 1) * P], W("w2")[:, c * D:(c + 1) * D],
                                  start=(c == 0), stop=(c == CHUNKS - 1))
                    last.then_inc(f_ps, 1)

            pipeline(pe, feed, 2)


def position_table():
    pos = np.arange(S, dtype=np.float32)[:, None]
    div = np.exp(np.arange(0, D, 2, dtype=np.float32) * np.float32(-math.log(10000.0) / D)).astype(np.float32)
    ang = pos * div
    plus = np.stack([np.sin(ang), np.cos(ang)], axis=-1).reshape(S, D)
    minus = np.stack([np.sin(-ang), np.cos(-ang)], axis=-1).reshape(S, D)
    return np.concatenate([plus[::-1], minus[1:]], axis=0).astype(np.float32)


def shape_tables():
    p = np.arange(P)
    f = lambda a: np.ascontiguousarray(a, dtype=np.float32)
    e = np.arange(EXPERTS)
    return {
        "pe": f(position_table().T),
        "ident": f(np.eye(P)),
        "blk32": f((p[:, None] % 32) // HD == np.arange(32)[None] // HD),
        "blk128": f(p[:, None] // HD == p[None] // HD),
        "head16": f(p[:, None] // HD == np.arange(HEADS)[None]),
        "vmask": f(p[:, None] // S == np.arange(32)[None] // HD),
        "ones4": f(p[:, None] // S == np.arange(4)[None]),
        "batch_row": f(p[:, None] % BT == p[None] // S),
        "batch_tile": f(p[:, None] // BT == np.arange(TILES)[None]),
        "lower": f(np.broadcast_to((e[None, :] < e[:, None]).reshape(1, -1), (P, EXPERTS * EXPERTS))),
    }


def kernel(**inputs):
    import concourse.bacc as bacc
    from concourse.bass_utils import run_bass_kernel_spmd

    a = {k: np.asarray(v) for k, v in inputs.items()}
    X, A, F = "L0_xattn_", "L0_attn_", "L0_ffn_"

    def experts(name):
        return np.concatenate([a[F + "routed_" + name].transpose(1, 0, 2).reshape(D, FR),
                               a[F + "shared_" + name].transpose(1, 0, 2).reshape(D, FS)], axis=1)

    w2 = np.concatenate([a[F + "routed_w2"].reshape(FR, D), a[F + "shared_w2"].reshape(FS, D)], axis=0)
    col = lambda name: a[name].reshape(P, 1)
    parts = {
        "xwq": a[X + "wq_w"].T, "xwk": a[X + "wk_w"].T, "xwv": a[X + "wv_w"].T, "xwo": a[X + "wo_w"].T,
        "awq": a[A + "Wq"].T, "awk": a[A + "Wk"].T, "awv": a[A + "Wv"].T, "awp": a[A + "Wpos"].T, "awo": a[A + "Wout"].T,
        "w1": experts("w1"), "w3": experts("w3"),
        "w2": w2.reshape(CHUNKS, P, D).transpose(1, 0, 2).reshape(P, FF), "router": a[F + "router_w"],
        "xbq": col(X + "wq_b"), "xbk": col(X + "wk_b"), "xbv": col(X + "wv_b"), "abq": col(A + "bq"), "abk": col(A + "bk"),
        "u": col(A + "u_bias"), "v": col(A + "v_bias"), "gamma": col(A + "ln_gamma"), "beta": col(A + "ln_beta"),
        **shape_tables(),
    }
    weights = np.ascontiguousarray(np.concatenate([parts[n] for n, _ in WEIGHT_BLOCKS], axis=1))
    vectors = {"xbv": a[X + "wv_b"], "xbo": a[X + "wo_b"], "ln_g": a[X + "ln_g"], "ln_b": a[X + "ln_b"],
               "abv": a[A + "bv"], "abo": a[A + "bout"], "rb": a[F + "router_b"]}
    rows = np.ascontiguousarray(np.concatenate([vectors[n] for n, _ in ROW_BLOCKS]))
    c = a["ctx_1024"]
    ctx_main = np.ascontiguousarray(c[:, :2 * P].reshape(TILES, BT, 2, P, D).transpose(0, 3, 1, 2, 4))
    ctx_last = np.ascontiguousarray(c[:, 2 * P].reshape(TILES, BT, D))
    mask = np.ascontiguousarray(a["mask_Bx1xSxS2_bf0"]).reshape(NB, S * S2)
    arrays = {"in_x": np.ascontiguousarray(a["x"]), "in_ctx_main": ctx_main, "in_ctx_last": ctx_last,
              "in_mask": mask, "in_weights": weights, "in_rows": rows}

    nc = bacc.Bacc("TRN2", target_bir_lowering=False, num_devices=1)
    f32 = mybir.dt.float32
    args = [nc.dram_tensor(n, v.shape, mybir.dt.from_np(v.dtype), kind="ExternalInput").ap() for n, v in arrays.items()]
    out = nc.dram_tensor("out_x", (NB, S, D), f32, kind="ExternalOutput").ap()
    pos_scratch = nc.dram_tensor("pos_scratch", (NB, S, HEADS * S), f32, kind="Internal").ap()
    v_scratch = nc.dram_tensor("v_scratch", (TILES, P, D), f32, kind="Internal").ap()
    perceiver_kernel(nc, *args, out, pos_scratch, v_scratch)
    r = run_bass_kernel_spmd(nc, [arrays], core_ids=[0])
    return r.results[0]["out_x"]
```

```python
import math

import numpy as np

import concourse.bass as bass
from concourse import mybir

NB, S, D = 128, 32, 128
S2 = 257
ARENA = 13900
HEADS, HD = 16, 8
P = 128
BT = P // S
TILES = NB // BT
GT = 4
PR = 4
PAIRS = HEADS // 2
HG = P // S
POS = 2 * S - 1
EXPERTS, HID, SHARED = 8, 64, 2
FR, FS = EXPERTS * HID, SHARED * HID
FF = FR + FS
CHUNKS = FF // P
SW = EXPERTS + 2 * FS
EPS = 1e-5
DK = float(np.float32(np.sqrt(np.float16(HD))) + np.float32(1e-8))
GW = D + 1
PIECES = 3
NP2 = PIECES * PIECES
OW = 36

WEIGHT_BLOCKS = [
    ("xwq", D), ("xwk", D), ("xwv", D), ("xwo", D),
    ("awq", D), ("awk", D), ("awv", D), ("awp", D), ("awo", D),
    ("xbq", 1), ("xbk", 1), ("xbv", 1), ("abq", 1), ("abk", 1), ("u", 1), ("v", 1), ("gamma", 1), ("beta", 1),
    ("pe", POS), ("ident", P), ("blk32", 32), ("blk128", P), ("head16", HEADS), ("vmask", 32), ("parity", 2), ("ones4", 4),
    ("batch_row", P), ("batch_tile", TILES), ("lower", EXPERTS * EXPERTS),
    ("w1", FR), ("w3", FR), ("shared", SW), ("w2", FF),
]
ROW_BLOCKS = [("xbv", D), ("xbo", D), ("ln_g", D), ("ln_b", D), ("abv", D), ("abo", D), ("rb", EXPERTS)]


def offsets(blocks):
    at, out = 0, {}
    for name, n in blocks:
        out[name] = (at, n)
        at += n
    return out, at


WEIGHT_AT, WEIGHT_COLS = offsets(WEIGHT_BLOCKS)
ROW_AT, ROW_COLS = offsets(ROW_BLOCKS)
EARLY_COLS = WEIGHT_AT["w1"][0]
EARLY_X, MORE_X = 4, 8


def perceiver_kernel(nc, x, ctx_main, ctx_last, mask, weights, rows, out, pos_scratch, v_scratch, piece_scratch):
    f32 = mybir.dt.float32
    bf16 = mybir.dt.bfloat16
    ALU = mybir.AluOpType
    ACT = mybir.ActivationFunctionType
    AX = mybir.AxisListType.X

    from contextlib import ExitStack

    ctx = ExitStack()
    with ctx:
        def sb(name, shape, dt=f32):
            return ctx.enter_context(nc.sbuf_tensor(name, shape, dt))

        def sem(name):
            return ctx.enter_context(nc.semaphore(name))

        w_sb = sb("w_sb", [P, WEIGHT_COLS])
        row_sb = sb("row_sb", [P, ROW_COLS])

        def W(name):
            at, n = WEIGHT_AT[name]
            return w_sb[:, at:at + n]

        def ROW(name):
            at, n = ROW_AT[name]
            return row_sb[:, at:at + n]

        x_all = sb("x_all", [P, TILES, D])
        q_all = sb("q_all", [P, NB, S])
        k_all = sb("k_all", [P, NB * S])
        half = sb("half", [P, 1])
        warm = sb("warm", [P, 1])
        calm = sb("calm", [P, P])
        poison = sb("poison", [P, TILES])
        cols = sb("cols", [P, 8])
        xbq_s, xbv_n, qv_b, qu_b = (cols[:, n:n + 1] for n in range(4))
        qu_bias = cols[:, 4:6]
        bk_heads = sb("bk_heads", [P, P])
        pos_blk = sb("pos_blk", [P, HEADS, POS])
        mask_sb = sb("mask_sb", [P, S * S2 // 4])
        pos_st = mask_sb[:, 0:PR * HEADS * S].rearrange("p (r n) -> p r n", r=PR)
        cl_piece = sb("cl_piece", [P, PIECES, GW], bf16)
        flag = sb("flag", [P, 2])
        flag_tile = sb("flag_tile", [P, TILES])
        k_blk = sb("k_blk", [P, 2, PAIRS, GT * P])
        v_blk = sb("v_blk", [P, 2, BT, HG, OW])

        arena = sb("arena", [P, ARENA])

        def phase():
            at = [0]

            def part(name, shape):
                n = int(np.prod(shape[1:]))
                assert at[0] + n <= ARENA, name
                flat = arena[0:shape[0], at[0]:at[0] + n]
                at[0] += n
                names = [f"d{k}" for k in range(len(shape) - 1)]
                if len(names) == 1:
                    return flat
                return flat.rearrange(f"p ({' '.join(names)}) -> p {' '.join(names)}", **dict(zip(names[1:], shape[2:])))
            return part

        cross_part, attend_part, feed_part = phase(), phase(), phase()

        c_sb = cross_part("c_sb", [P, 2, BT, 2, GW])
        clw = cross_part("clw", [NP2, 2, BT * GW // 2]).bitcast(bf16).rearrange("p s (b n) -> p s b n", b=BT)
        clm = cross_part("clm", [NP2, 2, BT * GW // 2]).bitcast(bf16).rearrange("p s (b n) -> p s b n", b=BT)
        cl_all = cross_part("cl_all", [P, D])
        cl_rest = cross_part("cl_rest", [P, 2, D])
        st1 = cross_part("st1", [P, 2, 6])
        mv1 = cross_part("mv1", [P, 2, 2])
        rs1 = cross_part("rs1", [P, 2])
        ve1 = cross_part("ve1", [P, 2])
        x1 = cross_part("x1", [P, 2, D])
        x1b = cross_part("x1b", [P, TILES, D])
        x1t = cross_part("x1t", [P, 2, P])
        qt = cross_part("qt", [P, 2, P])
        g_sb = cross_part("g_sb", [P, 2, BT, GW])
        t_sb = cross_part("t_sb", [P, 2, BT, D])
        m_sb = cross_part("m_sb", [P, 2, BT, 32])
        vs_sb = cross_part("vs_sb", [P, 2, BT])
        rv_sb = cross_part("rv_sb", [P, 2, P])
        ct_sb = cross_part("ct_sb", [P, 2, P])
        y_sb = cross_part("y_sb", [P, 2, D])
        stn = cross_part("stn", [P, 2, 6])
        mvn = cross_part("mvn", [P, 2, 2])
        rsn = cross_part("rsn", [P, 2])
        ven = cross_part("ven", [P, 2])
        yn = cross_part("yn", [P, 2, D])
        fin = cross_part("fin", [P, 2, D])
        fin2 = cross_part("fin2", [P, 2, D])
        st2 = cross_part("st2", [P, 2, 6])
        mv2 = cross_part("mv2", [P, 2, 2])
        rs2 = cross_part("rs2", [P, 2])
        ve2 = cross_part("ve2", [P, 2])
        xn = cross_part("xn", [P, 2, D])
        xnt = cross_part("xnt", [P, 2, P])
        v_st = cross_part("v_st", [P, 2, D])
        qv = sb("qv", [P, PR, NB])
        pos_sb = attend_part("pos_sb", [P, 2, GT, HEADS * S])
        v_rep = attend_part("v_rep", [P, 2, GT * BT, D])
        qu = attend_part("qu", [P, 2, 2, P])
        sc = attend_part("sc", [P, 2, HEADS * S])
        mx = attend_part("mx", [P, 2, HEADS])
        z_sb = attend_part("z_sb", [P, 2, HEADS * S])
        e_sb = attend_part("e_sb", [P, 2, HEADS * S])
        et = attend_part("et", [P, 2, HG, P])
        rden = attend_part("rden", [P, 2, HG, HG])
        cn = attend_part("cn", [P, 2, D])
        cnt = attend_part("cnt", [P, 2, P])
        st3 = feed_part("st3", [P, 2, 6])
        mv3 = feed_part("mv3", [P, 2, 2])
        ve3 = feed_part("ve3", [P, 2])
        rs3 = feed_part("rs3", [P, 2])
        x3 = feed_part("x3", [P, 2, D])
        x3t = feed_part("x3t", [P, 2, P])
        lg = feed_part("lg", [P, 2, EXPERTS])
        m8 = feed_part("m8", [P, 2, 8])
        dz = feed_part("dz", [P, 2])
        th = feed_part("th", [P, 2])
        side = feed_part("side", [P, 2, EXPERTS])
        share = feed_part("share", [P, 2, EXPERTS])
        cmp_gt = feed_part("cmp_gt", [P, 2, EXPERTS, EXPERTS])
        cmp_eq = feed_part("cmp_eq", [P, 2, EXPERTS, EXPERTS])
        rank = feed_part("rank", [P, 2, EXPERTS])
        gates = feed_part("gates", [P, 2, EXPERTS])
        sg = feed_part("sg", [P, 2, FF])
        sgg = feed_part("sgg", [P, 2, FR])
        hh = feed_part("hh", [P, 2, FF])
        ht = feed_part("ht", [P, 2, FF])

        bank = [ctx.enter_context(nc.psum_tensor(f"bank{n}", [P, 512], f32)) for n in range(8)]

        weights_in, rows_in, late_weights_in = sem("weights_in"), sem("rows_in"), sem("late_weights_in")
        x_in, more_x_in, late_x_in, mask_in = sem("x_in"), sem("more_x_in"), sem("late_x_in"), sem("mask_in")
        ctx_in = [sem("ctx_in0"), sem("ctx_in1")]
        half_set, ones_set, last_ones_set, zeros_set = sem("half_set"), sem("ones_set"), sem("last_ones_set"), sem("zeros_set")
        calm_set = sem("calm_set")
        last_in, piece_done, rest_done, pieces_stored = sem("last_in"), sem("piece_done"), sem("rest_done"), sem("pieces_stored")
        cols_set, flag_set, ftile_set, poison_sum, poison_set = (
            sem("cols_set"), sem("flag_set"), sem("ftile_set"), sem("poison_sum"), sem("poison_set"))
        pos_keys, pos_blk_set, bk_set = sem("pos_keys"), sem("pos_blk_set"), sem("bk_set")
        st1_done, mv1_done, ve1_done, rs1_done, x1_done = (sem(n) for n in ("st1_done", "mv1_done", "ve1_done", "rs1_done", "x1_done"))
        x1b_done = sem("x1b_done")
        xt_ps, xt_done, qt_ps, qt_done, r_ps, g_ps, g_done = (
            sem(n) for n in ("xt_ps", "xt_done", "qt_ps", "qt_done", "r_ps", "g_ps", "g_done"))
        t_ps, t_done, vs_ps, vs_done, rv_done, m_ps, m_done = (
            sem(n) for n in ("t_ps", "t_done", "vs_ps", "vs_done", "rv_done", "m_ps", "m_done"))
        c_ps, ct_done, y_ps, y_done = (sem(n) for n in ("c_ps", "ct_done", "y_ps", "y_done"))
        stn_done, mvn_done, ven_done, rsn_done, yn_done, fin_mul, fin_add, x_new = (
            sem(n) for n in ("stn_done", "mvn_done", "ven_done", "rsn_done", "yn_done", "fin_mul", "fin_add", "x_new"))
        st2_done, mv2_done, ve2_done, rs2_done, xn_done = (sem(n) for n in ("st2_done", "mv2_done", "ve2_done", "rs2_done", "xn_done"))
        xnt_ps, xnt_done, qk_ps, q_done, k_done, v_ps, v_done = (
            sem(n) for n in ("xnt_ps", "xnt_done", "qk_ps", "q_done", "k_done", "v_ps", "v_done"))
        v_stored = [sem("v_stored0"), sem("v_stored1")]
        qv_done, p_ps, p_done = sem("qv_done"), sem("p_ps"), sem("p_done")
        pos_stored = [sem(f"pos_stored{r}") for r in range(PR)]
        pos_first = [sem(f"pos_first{t}") for t in range(GT)]
        pos_in = [sem("pos_in0"), sem("pos_in1")]
        vrep_in = [sem("vrep_in0"), sem("vrep_in1")]
        kblk_in = [sem("kblk_in0"), sem("kblk_in1")]
        vblk_done, xb_done, qu_done, s_ps, sc_done, mx_done, z_done, e_done = (
            sem(n) for n in ("vblk_done", "xb_done", "qu_done", "s_ps", "sc_done", "mx_done", "z_done", "e_done"))
        et_ps, et_done, o_ps, rden_done, cn_done, cnt_ps, cnt_done, a_ps, x_att = (
            sem(n) for n in ("et_ps", "et_done", "o_ps", "rden_done", "cn_done", "cnt_ps", "cnt_done", "a_ps", "x_att"))
        st3_done, mv3_done, ve3_done, rs3_done, x3_done = (sem(n) for n in ("st3_done", "mv3_done", "ve3_done", "rs3_done", "x3_done"))
        x3t_ps, x3t_done, shared_ps, w1_ps, w3_ps, sg_done = (
            sem(n) for n in ("x3t_ps", "x3t_done", "shared_ps", "w1_ps", "w3_ps", "sg_done"))
        lg_done, m8_done, dz_done, th_done, side_done, share_done, gt_done, eq_done, eql_done, cmp_done, rank_done, gates_done = (
            sem(n) for n in ("lg_done", "m8_done", "dz_done", "th_done", "side_done", "share_done", "gt_done", "eq_done",
                             "eql_done", "cmp_done", "rank_done", "gates_done"))
        sgg_done, h_done, ht_ps, ht_done, f_ps, x_out = (
            sem(n) for n in ("sgg_done", "h_done", "ht_ps", "ht_done", "f_ps", "x_out"))
        out_stored = [sem("out_stored0"), sem("out_stored1")]

        x_tok = x.rearrange("(t b) s d -> (b s) t d", b=BT)
        out_tok = out.rearrange("(t b) s d -> t (b s) d", b=BT)

        def at(buf, t):
            return buf[:, bass.ds(t, 1), :].rearrange("p o n -> p (o n)")

        def dram_at(ap, t):
            return ap[bass.ds(t, 1)].rearrange("o p n -> (o p) n")

        def pipeline(eng, step, depth, unroll=2):
            peel = -(-depth // unroll) * unroll
            for i in range(peel):
                step(i, i % unroll, lambda k, i=i: i >= k)
            with eng.Fori(0, (TILES - peel) // unroll) as turn:
                for n in range(unroll):
                    step(unroll * turn + (peel + n), n, lambda k: True)
            for i in range(TILES, TILES + depth):
                step(i, i % unroll, lambda k, i=i: i - k < TILES)

        def rounds(eng, body, total, ring=2):
            for slot in range(ring):
                body(slot, slot, True)
            with eng.Fori(0, total // ring - 1) as turn:
                for slot in range(ring):
                    body(ring * turn + (ring + slot), slot, False)

        def loads_in(t, slot, n, ring=2):
            return t * (16 // ring * n) + (16 * n - 16 // ring * n * slot)

        def group_in(t, m, n):
            return (t - m) * (2 * n) + 16 * n

        def cap(count):
            return min(count, TILES) if isinstance(count, int) else count

        def draining(i):
            return isinstance(i, int) and i >= TILES

        def is_step(i, n):
            return isinstance(i, int) and i == n

        def load_keys(eng, t, slot, m):
            r = slice(2 * HD * m, 2 * HD * m + 2 * HD)
            eng.dma_start(k_blk[r, slot, m, :], k_all[r, bass.ds(t * P, GT * P)]).then_inc(kblk_in[slot], 16)

        block = ctx.enter_context(nc.Block())

        @block.sync
        def _(sp):
            sp.dma_start(cl_all[:], ctx_last).then_inc(last_in, 16)
            sp.dma_start(x_all[:, 0:EARLY_X, :], x_tok[:, 0:EARLY_X, :]).then_inc(x_in, 16)
            sp.dma_start(w_sb[:, 0:EARLY_COLS], weights[:, 0:EARLY_COLS]).then_inc(weights_in, 16)

            def load_context(i, slot, on):
                if on(0):
                    if is_step(i, 0):
                        sp.wait_ge(piece_done, PIECES)
                    if on(2):
                        sp.wait_ge(g_ps, 2 * i - 2)
                    sp.dma_start(c_sb[:, slot, :, :, 0:D], ctx_main[bass.ds(i, 1)].rearrange("o p b c d -> (o p) b c d")).then_inc(ctx_in[slot], 16)
                    if is_step(i, 0):
                        sp.dma_start(row_sb[:], rows.partition_broadcast(P)).then_inc(rows_in, 16)
                        sp.wait_ge(pieces_stored, 16)
                    pieces = piece_scratch[:, bass.ds(i * BT, BT), :].rearrange("k b n -> k (b n)")
                    sp.dma_start(clw[:, slot], pieces.unsqueeze(1).broadcast_to([PIECES, PIECES, BT * GW])).then_inc(ctx_in[slot], 16)
                    sp.dma_start(clm[:, slot], pieces.unsqueeze(0).broadcast_to([PIECES, PIECES, BT * GW])).then_inc(ctx_in[slot], 16)
                if is_step(i, 0):
                    sp.dma_start(mask_sb[:].bitcast(mybir.dt.uint8), mask).then_inc(mask_in, 16)
                if is_step(i, 1):
                    sp.dma_start(x_all[:, EARLY_X:MORE_X, :], x_tok[:, EARLY_X:MORE_X, :]).then_inc(more_x_in, 16)
                if is_step(i, 3):
                    sp.dma_start(x_all[:, MORE_X:, :], x_tok[:, MORE_X:, :]).then_inc(late_x_in, 16)
                if is_step(i, 5):
                    sp.dma_start(w_sb[:, EARLY_COLS:], weights[:, EARLY_COLS:]).then_inc(late_weights_in, 16)
                if on(8):
                    sp.wait_ge(v_done, i - 7)
                    sp.dma_start(v_scratch[:, bass.ds(i - 8, 1)].rearrange("j o b d -> b j (o d)"), v_st[:, slot, :]).then_inc(v_stored[slot], 16)

            sp.wait_ge(ones_set, 1)
            pipeline(sp, load_context, 8)

            pos_tok = pos_scratch.rearrange("(t b) i n -> t (b i) n", b=BT)
            v_tok = v_scratch.rearrange("j t b d -> j (t b d)").unsqueeze(0)

            def store_position(i, slot):
                sp.wait_ge(p_done, i + 1 + PR)
                sp.dma_start(pos_scratch[:, bass.ds(i, 1), :].rearrange("b o n -> b (o n)"), pos_st[:, slot, :]).then_inc(pos_stored[slot], 16)

            def load_values(g, slot):
                sp.dma_start(v_rep[:, slot, :, :].rearrange("p b d -> p (b d)"),
                             v_tok[:, :, bass.ds(g * (GT * BT * D), GT * BT * D)].broadcast_to([HG, S, GT * BT * D])).then_inc(vrep_in[slot], 16)

            for s in range(2):
                sp.wait_ge(v_stored[s], 16 * TILES // 2)
            sp.wait_ge(k_done, TILES)
            load_values(0, 0)
            with sp.Fori(0, S // PR) as turn:
                for slot in range(PR):
                    store_position(PR * turn + slot, slot)
            for s in range(PR):
                sp.wait_ge(pos_stored[s], 16 * S // PR)
            sp.wait_ge(zeros_set, 2)

            def load_group(g, slot, first):
                if not first:
                    sp.wait_ge(sc_done, GT * g - GT)
                if is_step(g, 0):
                    for t in range(GT):
                        sp.dma_start(pos_sb[:, slot, t, :], pos_tok[t]).then_inc(pos_first[t], 16)
                    return
                sp.dma_start(pos_sb[:, slot, :, :], pos_tok[bass.ds(g * GT, GT)].rearrange("t p n -> p t n")).then_inc(pos_in[slot], 16)
                if not first:
                    sp.wait_ge(s_ps, GT * g - GT)
                for m in range(PAIRS):
                    load_keys(sp, g * GT, slot, m)
                if not first:
                    sp.wait_ge(vblk_done, GT * g - GT)
                load_values(g, slot)

            rounds(sp, load_group, TILES // GT)

            with sp.Fori(0, TILES // 2) as pair:
                for slot in range(2):
                    t = 2 * pair + slot
                    sp.wait_ge(x_out, t + 1)
                    sp.dma_start(dram_at(out_tok, t), at(x_all, t)).then_inc(out_stored[slot], 16)
            for s in range(2):
                sp.wait_ge(out_stored[s], 16 * TILES // 2)

        @block.gpsimd
        def _(pool):
            pool.memset(calm[:], 0.0).then_inc(calm_set, 1)
            pool.memset(half[:], -0.5).then_inc(half_set, 1)
            pool.memset(c_sb[:, :, :, :, D:GW], 1.0).then_inc(ones_set, 1)
            pool.memset(cl_piece[:, 0:1, D:GW], 1.0).then_inc(last_ones_set, 1)
            pool.memset(cl_piece[:, 1:PIECES, D:GW], 0.0).then_inc(last_ones_set, 1)
            pool.wait_ge(half_set, 1)

            def cross(i, slot, on):
                other = (slot + 1) % 2
                if on(5):
                    pool.wait_ge(yn_done, i - 4)
                    pool.tensor_tensor(fin[:, other, :], yn[:, other, :], ROW("ln_g"), ALU.mult).then_inc(fin_mul, 1)
                    pool.wait_ge(fin_mul, i - 4)
                    pool.tensor_tensor(fin2[:, other, :], fin[:, other, :], ROW("ln_b"), ALU.add).then_inc(fin_add, 1)
                    pool.wait_ge(fin_add, i - 4)
                    pool.tensor_tensor(at(x_all, i - 5), at(x_all, i - 5), fin2[:, other, :], ALU.add).then_inc(x_new, 1)
                if on(6):
                    pool.wait_ge(ve2_done, i - 5)
                    pool.tensor_tensor(rs2[:, slot:slot + 1], ve2[:, slot:slot + 1], half[:], ALU.pow).then_inc(rs2_done, 1)
                if on(0):
                    pool.wait_ge(ve1_done, i + 1)
                    pool.tensor_tensor(rs1[:, slot:slot + 1], ve1[:, slot:slot + 1], half[:], ALU.pow).then_inc(rs1_done, 1)
                if on(4):
                    pool.wait_ge(ven_done, i - 3)
                    pool.tensor_tensor(rsn[:, slot:slot + 1], ven[:, slot:slot + 1], half[:], ALU.pow).then_inc(rsn_done, 1)
                if is_step(i, 1):
                    pool.wait_ge(rows_in, 16)
                if on(1):
                    pool.wait_ge(x1_done, i)
                    pool.tensor_tensor(at(x1b, i - 1), x1[:, other, :], ROW("xbo"), ALU.add).then_inc(x1b_done, 1)
                if is_step(i, 1) or is_step(i, 2):
                    pool.memset(k_blk[:, i - 1], 0.0).then_inc(zeros_set, 1)

            pipeline(pool, cross, 6)

            pool.wait_ge(ct_done, TILES)

            for s in range(2):
                pool.tensor_copy(v_blk[:, s, :, :, 32:OW].rearrange("p b g o -> p (b g) o"),
                                 W("ones4").unsqueeze(1).broadcast_to([P, BT * HG, 4])).then_inc(zeros_set, 1)

            pool.wait_ge(x_new, TILES)
            pool.wait_ge(xn_done, TILES)

            def spread(t, n, on):
                slot, group, r = n % 2, n // GT, n % GT
                if r == 0:
                    pool.wait_ge(vrep_in[group], group_in(t, n, 1))
                if on(2):
                    pool.wait_ge(o_ps, t - 1)
                pool.tensor_tensor(v_blk[:, slot, :, :, 0:32], v_rep[:, group, BT * r:BT * r + BT, :].rearrange("p b (g n) -> p b g n", g=HG),
                                   W("vmask").unsqueeze(1).unsqueeze(1).broadcast_to([P, BT, HG, 32]), ALU.mult).then_inc(vblk_done, 1)
                pool.tensor_tensor(at(x_all, t), at(x_all, t), ROW("abo"), ALU.add).then_inc(xb_done, 1)

            for t in range(2 * GT):
                spread(t, t, lambda k, t=t: t >= k)
            with pool.Fori(0, TILES // (2 * GT) - 1) as turn:
                for n in range(2 * GT):
                    spread(2 * GT * turn + (2 * GT + n), n, lambda k: True)

            def gate(i, slot, on):
                if on(0):
                    pool.wait_ge(ve3_done, i + 1)
                    pool.tensor_tensor(rs3[:, slot:slot + 1], ve3[:, slot:slot + 1], half[:], ALU.pow).then_inc(rs3_done, 1)
                if on(2):
                    pool.wait_ge(sg_done, i - 1)
                    pool.wait_ge(gates_done, i - 1)
                    pool.tensor_tensor(sgg[:, slot, :].rearrange("p (e n) -> p e n", e=EXPERTS), sg[:, slot, 0:FR].rearrange("p (e n) -> p e n", e=EXPERTS),
                                       gates[:, slot, :].unsqueeze(2).broadcast_to([P, EXPERTS, HID]), ALU.mult).then_inc(sgg_done, 1)

            pipeline(pool, gate, 2)

        @block.scalar
        def _(act):
            act.wait_ge(half_set, 1)
            act.wait_ge(piece_done, PIECES)
            act.wait_ge(last_ones_set, 2)
            act.dma_start(piece_scratch.rearrange("k b n -> b k n"), cl_piece[:]).then_inc(pieces_stored, 16)
            act.activation(warm[:], half[:], ACT.Copy)
            act.wait_ge(weights_in, 16)
            act.wait_ge(cols_set, 5)

            def cross(i, slot, on):
                if on(0):
                    act.wait_ge(xt_ps, i + 1)
                    act.activation(x1t[:, slot, :], bank[0][:, 0:P], ACT.Copy).then_inc(xt_done, 1)
                    if on(2):
                        act.wait_ge(vs_ps, i - 1)
                    act.wait_ge(g_ps, 2 * i + 1)
                    act.activation(g_sb[:, slot, 0:2, :], bank[2][:, 0:2 * GW].rearrange("p (b n) -> p b n", b=2), ACT.Copy).then_inc(g_done, 1)
                    if on(2):
                        act.wait_ge(c_ps, i - 1)
                    act.wait_ge(qt_ps, i + 1)
                    act.activation(qt[:, slot, :], bank[0][:, P:2 * P], ACT.Identity, bias=xbq_s, scale=1.0 / DK).then_inc(qt_done, 1)
                if on(5):
                    s = (slot + 1) % 2
                    if on(7):
                        act.wait_ge(v_ps, i - 6)
                        act.wait_ge(qk_ps, i - 6)
                    act.wait_ge(xnt_ps, i - 4)
                    act.activation(xnt[:, s, :], bank[0 if draining(i) else 7][:, 0:P], ACT.Identity, bias=W("beta"), scale=W("gamma")).then_inc(xnt_done, 1)
                if on(0):
                    act.wait_ge(g_ps, 2 * i + 2)
                    act.activation(g_sb[:, slot, 2:4, :], bank[3][:, 0:2 * GW].rearrange("p (b n) -> p b n", b=2), ACT.Copy).then_inc(g_done, 1)
                if on(5):
                    act.wait_ge(qk_ps, i - 4)
                    act.activation(q_all[:, bass.ds((i - 5) * BT, BT), :].rearrange("p b s -> p (b s)"), bank[7][:, P:2 * P], ACT.Copy).then_inc(q_done, 1)
                    act.activation(k_all[:, bass.ds((i - 5) * P, P)], bank[7][:, 2 * P:3 * P], ACT.Identity, bias=W("abk")).then_inc(k_done, 1)

            pipeline(act, cross, 7)

            act.wait_ge(q_done, TILES)
            act.wait_ge(k_done, TILES)
            act.wait_ge(zeros_set, 2)

            def query_position(i, slot):
                act.wait_ge(p_ps, i + 1)
                act.activation(qv[:, slot, :], q_all[:, :, bass.ds(i, 1)].rearrange("p b o -> p (b o)"), ACT.Identity, bias=qv_b).then_inc(qv_done, 1)

            for i in range(PAIRS):
                query_position(i, i % PR)
                load_keys(act, 0, 0, i)
            with act.Fori(0, (S - PAIRS) // PR) as turn:
                for slot in range(PR):
                    query_position(PR * turn + (PAIRS + slot), slot)
            act.activation(warm[:], half[:], ACT.Exp)

            def attend(i, n, on):
                slot, other = n % 2, (n + 1) % 2
                if on(0):
                    if on(2):
                        act.wait_ge(s_ps, i - 1)
                    for e in range(2):
                        last = act.activation(qu[:, slot, e, :], q_all[:, bass.ds(i * BT, BT), :].rearrange("p b s -> p (b s)"), ACT.Identity,
                                              bias=qu_bias[:, e:e + 1], scale=W("parity")[:, e:e + 1])
                    last.then_inc(qu_done, 1)
                if on(2):
                    act.wait_ge(z_done, i - 1)
                    if on(4):
                        act.wait_ge(et_ps, i - 3)
                    act.activation(e_sb[:, slot, :], z_sb[:, slot, :], ACT.Exp, scale=1.0 / math.sqrt(HD)).then_inc(e_done, 1)
                if on(5):
                    act.wait_ge(cnt_ps, i - 4)
                    if on(7):
                        act.wait_ge(a_ps, i - 6)
                    act.activation(cnt[:, other, :], bank[5][:, 0:P], ACT.Copy).then_inc(cnt_done, 1)
                if on(3):
                    act.wait_ge(et_ps, i - 2)
                    if on(5):
                        act.wait_ge(o_ps, i - 4)
                    act.activation(et[:, other, :, :].rearrange("p g n -> p (g n)"), bank[2 + other][:, :], ACT.Copy).then_inc(et_done, 1)

            pipeline(act, attend, 7)
            act.activation(warm[:], half[:], ACT.Silu)

            def feed(i, slot, on):
                other = (slot + 1) % 2
                if on(3):
                    act.wait_ge(ht_ps, i - 2)
                    if on(5):
                        act.wait_ge(f_ps, i - 4)
                    act.activation(ht[:, other, 0:512], bank[3][:, :], ACT.Copy)
                    act.activation(ht[:, other, 512:FF], bank[6][:, P:2 * P], ACT.Copy).then_inc(ht_done, 1)
                if on(1):
                    if on(3):
                        act.wait_ge(h_done, i - 2)
                        act.wait_ge(sgg_done, i - 2)
                    act.wait_ge(dz_done, i)
                    act.activation(th[:, other:other + 1], dz[:, other:other + 1], ACT.Tanh, scale=0.5).then_inc(th_done, 1)
                    act.wait_ge(shared_ps, i)
                    act.activation(sg[:, other, FR:FF], bank[2 + 2 * other][:, EXPERTS:EXPERTS + FS], ACT.Silu)
                    act.wait_ge(w1_ps, i)
                    act.activation(sg[:, other, 0:FR], bank[0][:, :], ACT.Silu).then_inc(sg_done, 1)
                if on(0):
                    act.wait_ge(x3t_ps, i + 1)
                    if on(2):
                        act.wait_ge(w3_ps, i - 1)
                    act.activation(x3t[:, slot, :], bank[6][:, 0:P], ACT.Copy).then_inc(x3t_done, 1)

            pipeline(act, feed, 5)

        @block.vector
        def _(dve):
            dve.wait_ge(last_in, 16)
            left = cl_all[:]
            for k in range(PIECES):
                if k:
                    dve.wait_ge(piece_done, k)
                    dve.tensor_tensor(cl_rest[:, k - 1, :], left, cl_piece[:, k - 1, 0:D], ALU.subtract).then_inc(rest_done, 1)
                    left = cl_rest[:, k - 1, :]
                    dve.wait_ge(rest_done, k)
                dve.tensor_copy(cl_piece[:, k, 0:D], left).then_inc(piece_done, 1)
            dve.wait_ge(x_in, 16)

            def derived_columns():
                dve.wait_ge(weights_in, 16)
                dve.tensor_scalar(xbq_s, W("xbq"), 1.0 / DK, None, ALU.mult).then_inc(cols_set, 1)
                dve.tensor_scalar(xbv_n, W("xbv"), float(S2), None, ALU.mult).then_inc(cols_set, 1)
                dve.tensor_tensor(qu_b, W("abq"), W("u"), ALU.add).then_inc(cols_set, 1)
                dve.tensor_tensor(qv_b, W("abq"), W("v"), ALU.add).then_inc(cols_set, 1)
                dve.wait_ge(cols_set, 4)
                dve.tensor_scalar(qu_bias, W("parity"), qu_b, None, ALU.mult).then_inc(cols_set, 1)
                dve.tensor_scalar(bk_heads[:], W("blk128"), W("xbk"), None, ALU.mult).then_inc(bk_set, 1)
                dve.wait_ge(cols_set, 5)

            def position_keys():
                dve.wait_ge(pos_keys, 1)
                dve.tensor_tensor(pos_blk[:], bank[7][:, 0:POS].unsqueeze(1).broadcast_to([P, HEADS, POS]),
                                  W("head16").unsqueeze(2).broadcast_to([P, HEADS, POS]), ALU.mult).then_inc(pos_blk_set, 1)

            def mask_flags():
                dve.wait_ge(mask_in, 16)
                dve.tensor_reduce(flag[:, 0:1], mask_sb[:].bitcast(mybir.dt.int32), AX, ALU.max).then_inc(flag_set, 1)
                dve.wait_ge(flag_set, 1)
                dve.tensor_scalar(flag[:, 1:2], flag[:, 0:1], 0.0, None, ALU.is_gt).then_inc(flag_set, 1)
                dve.wait_ge(flag_set, 2)
                dve.tensor_scalar(flag_tile[:], W("batch_tile"), flag[:, 1:2], None, ALU.mult).then_inc(ftile_set, 1)

            def mask_poison():
                dve.wait_ge(poison_sum, 1)
                dve.tensor_scalar(poison[:], bank[6][:, 0:TILES], -3.0e38, 3.0e38, ALU.mult, ALU.mult).then_inc(poison_set, 1)
                dve.wait_ge(poison_set, 1)

            def cross(i, slot, on):
                other = (slot + 1) % 2
                if is_step(i, 1):
                    derived_columns()
                if is_step(i, 2):
                    position_keys()
                    dve.wait_ge(rows_in, 16)
                if on(1):
                    if on(3):
                        dve.wait_ge(xt_ps, i - 2)
                        dve.wait_ge(x1b_done, i - 2)
                    dve.wait_ge(rs1_done, i)
                    dve.tensor_scalar(x1[:, other, :], at(x_all, i - 1), mv1[:, other, 0:1], rs1[:, other:other + 1], ALU.subtract, ALU.mult).then_inc(x1_done, 1)
                if on(6):
                    dve.wait_ge(x_new, i - 5)
                    dve.bn_stats(st2[:, slot, :], at(x_all, i - 6)).then_inc(st2_done, 1)
                if is_step(i, EARLY_X):
                    dve.wait_ge(more_x_in, 16)
                if is_step(i, MORE_X):
                    dve.wait_ge(late_x_in, 16)
                if on(0):
                    dve.bn_stats(st1[:, slot, :], at(x_all, i)).then_inc(st1_done, 1)
                if on(6):
                    dve.wait_ge(st2_done, i - 5)
                    dve.nop(nofuse=True)
                    dve.bn_aggr(mv2[:, slot, :], st2[:, slot, :]).then_inc(mv2_done, 1)
                if on(0):
                    dve.wait_ge(st1_done, i + 1)
                    dve.nop(nofuse=True)
                    dve.bn_aggr(mv1[:, slot, :], st1[:, slot, :]).then_inc(mv1_done, 1)
                if on(6):
                    dve.wait_ge(mv2_done, i - 5)
                    dve.tensor_scalar(ve2[:, slot:slot + 1], mv2[:, slot, 1:2], 1.0 + EPS, EPS * EPS, ALU.mult, ALU.add).then_inc(ve2_done, 1)
                if on(0):
                    dve.wait_ge(mv1_done, i + 1)
                    dve.tensor_scalar(ve1[:, slot:slot + 1], mv1[:, slot, 1:2], 1.0, EPS, ALU.mult, ALU.add).then_inc(ve1_done, 1)
                if is_step(i, 4):
                    mask_poison()
                if on(4):
                    dve.wait_ge(y_ps, i - 3)
                    dve.wait_ge(x1b_done, i - 3)
                    dve.scalar_tensor_tensor(y_sb[:, slot, :], bank[6][:, 0:D], poison[:, bass.ds(i - 4, 1)], at(x1b, i - 4),
                                             ALU.add, ALU.add).then_inc(y_done, 1)
                    dve.wait_ge(y_done, i - 3)
                    dve.bn_stats(stn[:, slot, :], y_sb[:, slot, :]).then_inc(stn_done, 1)
                if on(6):
                    if on(8):
                        dve.wait_ge(xnt_ps, i - 7)
                    dve.wait_ge(rs2_done, i - 5)
                    dve.tensor_scalar(xn[:, slot, :], at(x_all, i - 6), mv2[:, slot, 0:1], rs2[:, slot:slot + 1], ALU.subtract, ALU.mult).then_inc(xn_done, 1)
                if on(4):
                    dve.wait_ge(stn_done, i - 3)
                    dve.nop(nofuse=True)
                    dve.bn_aggr(mvn[:, slot, :], stn[:, slot, :]).then_inc(mvn_done, 1)
                    dve.wait_ge(mvn_done, i - 3)
                    dve.tensor_scalar(ven[:, slot:slot + 1], mvn[:, slot, 1:2], 1.0, EPS, ALU.mult, ALU.add).then_inc(ven_done, 1)
                if on(3):
                    dve.wait_ge(m_ps, i - 2)
                    dve.tensor_tensor(m_sb[:, other, :, :], bank[5][:, 0:BT * 32].rearrange("p (b n) -> p b n", b=BT),
                                      W("blk32").unsqueeze(1).broadcast_to([P, BT, 32]), ALU.mult).then_inc(m_done, 1)
                if on(4):
                    if on(6):
                        dve.wait_ge(fin_mul, i - 5)
                    dve.wait_ge(rsn_done, i - 3)
                    dve.tensor_scalar(yn[:, slot, :], y_sb[:, slot, :], mvn[:, slot, 0:1], rsn[:, slot:slot + 1], ALU.subtract, ALU.mult).then_inc(yn_done, 1)
                if on(7):
                    dve.wait_ge(v_ps, i - 6)
                    if on(9):
                        dve.wait_ge(v_stored[other], loads_in(i - 9, other, 1))
                    dve.tensor_tensor(v_st[:, other, :], bank[6][:, P:2 * P], ROW("abv"), ALU.add).then_inc(v_done, 1)
                if is_step(i, 2):
                    mask_flags()
                if on(2):
                    dve.wait_ge(t_ps, i - 1)
                    for b in range(BT):
                        dve.scalar_tensor_tensor(t_sb[:, slot, b, :], ROW("xbv"), g_sb[:, slot, b, D:GW],
                                                 bank[4][:, b * D:(b + 1) * D], ALU.mult, ALU.add).then_inc(t_done, 1)
                    dve.wait_ge(vs_ps, i - 1)
                    dve.tensor_scalar(vs_sb[:, slot, :], bank[1][:, P:P + BT], xbv_n, None, ALU.add).then_inc(vs_done, 1)
                if on(3):
                    dve.wait_ge(c_ps, i - 2)
                    dve.wait_ge(rv_done, i - 2)
                    dve.tensor_tensor(ct_sb[:, other, :], bank[5][:, P:2 * P], rv_sb[:, other, :], ALU.add).then_inc(ct_done, 1)
                if on(2):
                    dve.wait_ge(vs_done, i - 1)
                    dve.wait_ge(r_ps, i - 1)
                    dve.tensor_tensor(rv_sb[:, slot, :].rearrange("p (b s) -> p b s", b=BT), bank[1][:, 0:P].rearrange("p (b s) -> p b s", b=BT),
                                      vs_sb[:, slot, :].unsqueeze(2).broadcast_to([P, BT, S]), ALU.mult).then_inc(rv_done, 1)

            pipeline(dve, cross, 9)

            dve.sem_inc(p_done, PR)

            def keep_positions(i, slot, first):
                dve.wait_ge(p_ps, i + 1 + PR)
                if not first:
                    dve.wait_ge(pos_stored[slot], loads_in(i - PR, slot, 1, PR))
                dve.tensor_copy(pos_st[:, slot, :], bank[slot][:, :]).then_inc(p_done, 1)

            rounds(dve, keep_positions, S, PR)

            def heads(ap):
                return ap.rearrange("p (h j) -> p h j", h=HEADS)

            def attend(i, n, on):
                slot, other = n % 2, (n + 1) % 2
                if on(5):
                    dve.wait_ge(a_ps, i - 4)
                    dve.wait_ge(xb_done, i - 4)
                    dve.tensor_tensor(at(x_all, i - 5), bank[6][:, 0:D], at(x_all, i - 5), ALU.add).then_inc(x_att, 1)
                if on(0):
                    dve.wait_ge(s_ps, i + 1)
                    if isinstance(i, int) and i < GT:
                        dve.wait_ge(pos_first[i], 16)
                    elif n % GT == 0:
                        dve.wait_ge(pos_in[n // GT], group_in(i, n, 1) - (16 if n < GT else 0))
                    dve.tensor_tensor(sc[:, slot, :], bank[slot][:, :], pos_sb[:, n // GT, n % GT, :], ALU.add).then_inc(sc_done, 1)
                if on(3):
                    dve.wait_ge(o_ps, i - 2)
                    dve.reciprocal(rden[:, other, :, :], bank[4][:, 0:HG * OW].rearrange("p (g n) -> p g n", g=HG)[:, :, 32:OW]).then_inc(rden_done, 1)
                if on(0):
                    dve.wait_ge(sc_done, i + 1)
                    dve.tensor_reduce(mx[:, slot, :], heads(sc[:, slot, :]), AX, ALU.max).then_inc(mx_done, 1)
                if on(3):
                    dve.wait_ge(rden_done, i - 2)
                    if on(5):
                        dve.wait_ge(cnt_ps, i - 4)
                    dve.tensor_tensor(cn[:, other, :].rearrange("p (g h n) -> p g h n", g=HG, h=HG),
                                      bank[4][:, 0:HG * OW].rearrange("p (g n) -> p g n", g=HG)[:, :, 0:32].rearrange("p g (h n) -> p g h n", h=HG),
                                      rden[:, other, :, :].unsqueeze(3).broadcast_to([P, HG, HG, HD]), ALU.mult).then_inc(cn_done, 1)
                if on(0):
                    dve.wait_ge(mx_done, i + 1)
                    if on(2):
                        dve.wait_ge(e_done, i - 1)
                    dve.tensor_tensor(heads(z_sb[:, slot, :]), heads(sc[:, slot, :]),
                                      mx[:, slot, :].unsqueeze(2).broadcast_to([P, HEADS, S]), ALU.subtract).then_inc(z_done, 1)

            pipeline(dve, attend, 5, 2 * GT)

            def feed(i, slot, on):
                other = (slot + 1) % 2
                L = lg[:, slot, :]
                mine = L.unsqueeze(2).broadcast_to([P, EXPERTS, EXPERTS])
                theirs = L.unsqueeze(1).broadcast_to([P, EXPERTS, EXPERTS])
                if on(5):
                    dve.wait_ge(f_ps, i - 4)
                    dve.tensor_tensor(at(x_all, i - 5), bank[5][:, 0:D], at(x_all, i - 5), ALU.add).then_inc(x_out, 1)
                if on(1):
                    if on(3):
                        dve.wait_ge(x3t_ps, i - 2)
                    dve.wait_ge(rs3_done, i)
                    dve.tensor_scalar(x3[:, other, :], at(x_all, i - 1), mv3[:, other, 0:1], rs3[:, other:other + 1], ALU.subtract, ALU.mult).then_inc(x3_done, 1)
                if on(2):
                    dve.wait_ge(shared_ps, i - 1)
                    dve.tensor_tensor(L, bank[2 + 2 * slot][:, 0:EXPERTS], ROW("rb"), ALU.add).then_inc(lg_done, 1)
                if on(3):
                    if on(5):
                        dve.wait_ge(ht_ps, i - 4)
                    dve.wait_ge(sg_done, i - 2)
                    dve.tensor_tensor(hh[:, other, FR:FF], bank[2 + 2 * other][:, EXPERTS + FS:SW], sg[:, other, FR:FF], ALU.mult)
                if on(2):
                    dve.wait_ge(lg_done, i - 1)
                    dve.nop(nofuse=True)
                    dve.max(m8[:, slot, :], L).then_inc(m8_done, 1)
                    dve.tensor_tensor(cmp_eq[:, slot], theirs, mine, ALU.is_equal).then_inc(eq_done, 1)
                    dve.wait_ge(m8_done, i - 1)
                    dve.tensor_tensor(dz[:, slot:slot + 1], m8[:, slot, 0:1], m8[:, slot, 1:2], ALU.subtract).then_inc(dz_done, 1)
                    dve.tensor_tensor(cmp_gt[:, slot], theirs, mine, ALU.is_gt).then_inc(gt_done, 1)
                    dve.wait_ge(eq_done, i - 1)
                    dve.tensor_tensor(cmp_eq[:, slot], cmp_eq[:, slot], W("lower").rearrange("p (a b) -> p a b", a=EXPERTS), ALU.mult).then_inc(eql_done, 1)
                if on(3):
                    dve.wait_ge(w3_ps, i - 2)
                    dve.wait_ge(sgg_done, i - 2)
                    dve.tensor_tensor(hh[:, other, 0:FR], bank[1 + 6 * other][:, :], sgg[:, other, :], ALU.mult).then_inc(h_done, 1)
                if on(2):
                    dve.wait_ge(eql_done, i - 1)
                    dve.wait_ge(gt_done, i - 1)
                    dve.tensor_tensor(cmp_gt[:, slot], cmp_gt[:, slot], cmp_eq[:, slot], ALU.add).then_inc(cmp_done, 1)
                if on(0):
                    if is_step(i, 0):
                        dve.wait_ge(x_att, TILES)
                    dve.bn_stats(st3[:, slot, :], at(x_all, i)).then_inc(st3_done, 1)
                if on(2):
                    dve.wait_ge(cmp_done, i - 1)
                    dve.tensor_reduce(rank[:, slot, :], cmp_gt[:, slot], AX, ALU.add).then_inc(rank_done, 1)
                if on(0):
                    dve.wait_ge(st3_done, i + 1)
                    dve.nop(nofuse=True)
                    dve.bn_aggr(mv3[:, slot, :], st3[:, slot, :]).then_inc(mv3_done, 1)
                if on(2):
                    dve.wait_ge(rank_done, i - 1)
                    dve.tensor_scalar(side[:, slot, :], rank[:, slot, :], -1.0, 0.5, ALU.mult, ALU.add).then_inc(side_done, 1)
                if on(0):
                    if on(2):
                        dve.wait_ge(rs3_done, i - 1)
                    dve.wait_ge(mv3_done, i + 1)
                    dve.tensor_scalar(ve3[:, slot:slot + 1], mv3[:, slot, 1:2], 1.0, EPS, ALU.mult, ALU.add).then_inc(ve3_done, 1)
                if on(2):
                    dve.wait_ge(side_done, i - 1)
                    dve.wait_ge(th_done, i - 1)
                    dve.tensor_scalar(share[:, slot, :], side[:, slot, :], th[:, slot:slot + 1], 0.5, ALU.mult, ALU.add).then_inc(share_done, 1)
                    dve.wait_ge(share_done, i - 1)
                    if on(4):
                        dve.wait_ge(sgg_done, i - 3)
                    dve.scalar_tensor_tensor(gates[:, slot, :], rank[:, slot, :], 2.0, share[:, slot, :], ALU.is_lt, ALU.mult).then_inc(gates_done, 1)

            pipeline(dve, feed, 5)

        @block.tensor
        def _(pe):
            mm = nc.tensor.matmul

            def keep_warm(n, count):
                for _ in range(count):
                    mm(bank[n][:, 0:P], calm[:], calm[:], start=True, stop=True)

            pe.wait_ge(calm_set, 1)
            keep_warm(6, 14)
            pe.wait_ge(weights_in, 16)
            ident = W("ident")
            mm(bank[7][:, 0:POS], W("awp"), W("pe"), start=True, stop=True).then_inc(pos_keys, 1)
            pe.wait_ge(bk_set, 1)

            def cross(j, slot, on):
                other = (slot + 1) % 2

                def gram(half):
                    g = bank[2 + half]
                    for n in range(2):
                        b = 2 * half + n
                        o = g[:, n * GW:(n + 1) * GW]
                        mm(o, c_sb[:, slot, b, 0, 0:D], c_sb[:, slot, b, 0, :], start=True, stop=False)
                        mm(o, c_sb[:, slot, b, 1, 0:D], c_sb[:, slot, b, 1, :], start=False, stop=False)
                        last = mm(o, clw[:, slot, b, 0:D], clm[:, slot, b, :], start=False, stop=True)
                    last.then_inc(g_ps, 1)

                if on(0):
                    pe.wait_ge(x1_done, j + 1)
                    nc.tensor.transpose(bank[0][:, 0:P], x1[:, slot, :], ident).then_inc(xt_ps, 1)
                    if is_step(j, 0):
                        keep_warm(6, 16)
                    pe.wait_ge(ctx_in[slot], loads_in(j, slot, 3))
                    gram(0)
                    pe.wait_ge(xt_done, j + 1)
                    mm(bank[0][:, P:2 * P], W("xwq"), x1t[:, slot, :], start=True, stop=True).then_inc(qt_ps, 1)
                if is_step(j, 5):
                    pe.wait_ge(pos_blk_set, 1)
                if on(5):
                    if on(6) and not draining(j):
                        pe.wait_ge(k_done, j - 5)
                    pe.wait_ge(xn_done, j - 4)
                    nc.tensor.transpose(bank[0 if draining(j) else 7][:, 0:P], xn[:, other, :], ident).then_inc(xnt_ps, 1)
                if on(2):
                    if on(6):
                        pe.wait_ge(v_done, j - 5)
                    if is_step(j, 2):
                        pe.wait_ge(ftile_set, 1)
                        mm(bank[6][:, 0:TILES], W("batch_row"), flag_tile[:], start=True, stop=True).then_inc(poison_sum, 1)
                        pe.wait_ge(poison_set, 1)
                    pe.wait_ge(ct_done, j - 1)
                    if on(3):
                        pe.wait_ge(y_done, j - 2)
                    mm(bank[6][:, 0:D], ct_sb[:, slot, :], W("xwo"), start=True, stop=True).then_inc(y_ps, 1)
                if on(0):
                    gram(1)
                    pe.wait_ge(qt_done, j + 1)
                    if on(1):
                        pe.wait_ge(rv_done, j)
                    mm(bank[1][:, 0:P], bk_heads[:], qt[:, slot, :], start=True, stop=True).then_inc(r_ps, 1)
                if on(5):
                    pe.wait_ge(xnt_done, j - 4)
                    mm(bank[7][:, P:2 * P], W("awq"), xnt[:, other, :], start=True, stop=True)
                    mm(bank[7][:, 2 * P:3 * P], W("awk"), xnt[:, other, :], start=True, stop=True).then_inc(qk_ps, 1)
                    pe.wait_ge(y_done, cap(j - 1))
                    if on(6):
                        pe.wait_ge(v_done, j - 5)
                    mm(bank[6][:, P:2 * P], xnt[:, other, :], W("awv"), start=True, stop=True).then_inc(v_ps, 1)
                if on(1):
                    if on(2):
                        pe.wait_ge(ct_done, j - 1)
                    pe.wait_ge(t_done, BT * j)
                    for g in range(HG):
                        last = mm(bank[5][32 * g:32 * g + 32, 0:BT * 32].rearrange("p (b n) -> p b n", b=BT), W("xwk")[:, 32 * g:32 * g + 32],
                                  t_sb[:, other, :, 32 * g:32 * g + 32], start=True, stop=True)
                    last.then_inc(m_ps, 1)
                if on(0):
                    for b in range(BT):
                        if b % 2 == 0:
                            pe.wait_ge(g_done, 2 * j + 1 + b // 2)
                        last = mm(bank[4][:, b * D:(b + 1) * D], g_sb[:, slot, b, 0:D], W("xwv"), start=True, stop=True)
                    last.then_inc(t_ps, 1)
                    mm(bank[1][:, P:P + BT], W("xwv"), g_sb[:, slot, :, D], start=True, stop=True).then_inc(vs_ps, 1)
                if on(1):
                    pe.wait_ge(m_done, j)
                    pe.nop(nofuse=True)
                    for b in range(BT):
                        for g in range(HG):
                            r = slice(32 * g, 32 * g + 32)
                            last = mm(bank[5][r, P + S * b:P + S * b + S], m_sb[r, other, b, :], qt[r, other, S * b:S * b + S], start=True, stop=True)
                    last.then_inc(c_ps, 1)

            pipeline(pe, cross, 5)

            pe.sem_inc(p_ps, PR)
            pe.wait_ge(ct_done, TILES)
            with pe.Fori(0, S // PR) as turn:
                for slot in range(PR):
                    i = PR * turn + slot
                    pe.wait_ge(qv_done, i + 1)
                    pe.wait_ge(p_done, i + 1)
                    pe.nop(nofuse=True)
                    mm(bank[slot][:, :].rearrange("p (h j) -> p h j", h=HEADS), qv[:, slot, :], pos_blk[:, :, bass.ds((S - 1 - slot) - PR * turn, S)],
                       start=True, stop=True).then_inc(p_ps, 1)

            pe.wait_ge(p_done, S + PR)
            pe.wait_ge(v_done, TILES)

            def attend(j, n, on):
                slot, other = n % 2, (n + 1) % 2
                if on(0):
                    pe.wait_ge(qu_done, j + 1)
                    if n % GT == 0:
                        pe.wait_ge(kblk_in[n // GT], group_in(j, n, PAIRS))
                    if on(2):
                        pe.wait_ge(sc_done, j - 1)
                    for e in range(2):
                        for b in range(BT):
                            last = mm(bank[slot][S * b:S * b + S, :].rearrange("p (m e j) -> p m e j", m=PAIRS, e=2)[:, :, e, :], qu[:, slot, e, S * b:S * b + S],
                                      k_blk[:, n // GT, :, P * (n % GT) + S * b:P * (n % GT) + S * b + S], start=True, stop=True)
                    last.then_inc(s_ps, 1)
                    if is_step(j, 1):
                        keep_warm(7, 29)
                if on(4):
                    pe.wait_ge(cn_done, j - 3)
                    if on(5):
                        pe.wait_ge(cnt_done, j - 4)
                    nc.tensor.transpose(bank[5][:, 0:P], cn[:, slot, :], ident).then_inc(cnt_ps, 1)
                if on(3):
                    pe.wait_ge(et_done, j - 2)
                    pe.wait_ge(vblk_done, j - 2)
                    if on(4):
                        pe.wait_ge(cn_done, j - 3)
                    for g in range(HG):
                        for b in range(BT):
                            last = mm(bank[4][S * b:S * b + S, g * OW:(g + 1) * OW], et[:, other, g, S * b:S * b + S],
                                      v_blk[:, other, b, g, :], start=True, stop=True)
                    last.then_inc(o_ps, 1)
                if on(1):
                    pe.wait_ge(e_done, j)
                    if on(3):
                        pe.wait_ge(et_done, j - 2)
                    for g in range(HG):
                        last = nc.tensor.transpose(bank[2 + other][:, g * P:(g + 1) * P], e_sb[:, other, g * P:(g + 1) * P], ident)
                    last.then_inc(et_ps, 1)
                if on(4):
                    pe.wait_ge(cnt_done, j - 3)
                    if on(5):
                        pe.wait_ge(x_att, j - 4)
                    mm(bank[6][:, 0:D], cnt[:, slot, :], W("awo"), start=True, stop=True).then_inc(a_ps, 1)

            pipeline(pe, attend, 4, 2 * GT)

            pe.wait_ge(x_att, TILES)
            pe.wait_ge(late_weights_in, 16)

            def feed(j, slot, on):
                other = (slot + 1) % 2
                if on(3):
                    pe.wait_ge(h_done, j - 2)
                    if on(4):
                        pe.wait_ge(ht_done, j - 3)
                    for c in range(4):
                        nc.tensor.transpose(bank[3][:, c * P:(c + 1) * P], hh[:, other, c * P:(c + 1) * P], ident)
                if on(1):
                    pe.wait_ge(x3t_done, cap(j))
                if on(3):
                    nc.tensor.transpose(bank[6][:, P:2 * P], hh[:, other, 4 * P:FF], ident).then_inc(ht_ps, 1)
                if on(1):
                    if on(3):
                        pe.wait_ge(h_done, j - 2)
                    mm(bank[2 + 2 * other][:, 0:SW], x3t[:, other, :], W("shared"), start=True, stop=True).then_inc(shared_ps, 1)
                    if on(2):
                        pe.wait_ge(sg_done, j - 1)
                    mm(bank[0][:, :], x3t[:, other, :], W("w1"), start=True, stop=True).then_inc(w1_ps, 1)
                    mm(bank[1 + 6 * other][:, :], x3t[:, other, :], W("w3"), start=True, stop=True).then_inc(w3_ps, 1)
                if on(3):
                    pe.wait_ge(ht_done, j - 2)
                if on(0):
                    pe.wait_ge(x3_done, j + 1)
                    nc.tensor.transpose(bank[6][:, 0:P], x3[:, slot, :], ident).then_inc(x3t_ps, 1)
                if on(3):
                    if on(4):
                        pe.wait_ge(x_out, j - 3)
                    for c in range(CHUNKS):
                        last = mm(bank[5][:, 0:D], ht[:, other, c * P:(c + 1) * P], W("w2")[:, c * D:(c + 1) * D],
                                  start=(c == 0), stop=(c == CHUNKS - 1))
                    last.then_inc(f_ps, 1)

            pipeline(pe, feed, 3)


def position_table():
    pos = np.arange(S, dtype=np.float32)[:, None]
    div = np.exp(np.arange(0, D, 2, dtype=np.float32) * np.float32(-math.log(10000.0) / D)).astype(np.float32)
    ang = pos * div
    plus = np.stack([np.sin(ang), np.cos(ang)], axis=-1).reshape(S, D)
    minus = np.stack([np.sin(-ang), np.cos(-ang)], axis=-1).reshape(S, D)
    return np.concatenate([plus[::-1], minus[1:]], axis=0).astype(np.float32)


def shape_tables():
    p = np.arange(P)
    f = lambda a: np.ascontiguousarray(a, dtype=np.float32)
    e = np.arange(EXPERTS)
    return {
        "pe": f(position_table().T),
        "ident": f(np.eye(P)),
        "blk32": f((p[:, None] % 32) // HD == np.arange(32)[None] // HD),
        "blk128": f(p[:, None] // HD == p[None] // HD),
        "head16": f(p[:, None] // HD == np.arange(HEADS)[None]),
        "parity": f((p[:, None] // HD) % 2 == np.arange(2)[None]),
        "vmask": f(p[:, None] // S == np.arange(32)[None] // HD),
        "ones4": f(p[:, None] // S == np.arange(4)[None]),
        "batch_row": f(p[:, None] % BT == p[None] // S),
        "batch_tile": f(p[:, None] // BT == np.arange(TILES)[None]),
        "lower": f(np.broadcast_to((e[None, :] < e[:, None]).reshape(1, -1), (P, EXPERTS * EXPERTS))),
    }


def kernel(**inputs):
    import concourse.bacc as bacc
    from concourse.bass_utils import run_bass_kernel_spmd

    a = {k: np.asarray(v) for k, v in inputs.items()}
    X, A, F = "L0_xattn_", "L0_attn_", "L0_ffn_"

    def routed(name):
        return a[F + "routed_" + name].transpose(1, 0, 2).reshape(D, FR)

    def shared(name):
        return a[F + "shared_" + name].transpose(1, 0, 2).reshape(D, FS)

    w2 = np.concatenate([a[F + "routed_w2"].reshape(FR, D), a[F + "shared_w2"].reshape(FS, D)], axis=0)
    col = lambda name: a[name].reshape(P, 1)
    parts = {
        "xwq": a[X + "wq_w"].T, "xwk": a[X + "wk_w"].T, "xwv": a[X + "wv_w"].T, "xwo": a[X + "wo_w"].T,
        "awq": a[A + "Wq"].T, "awk": a[A + "Wk"].T, "awv": a[A + "Wv"].T, "awp": a[A + "Wpos"].T, "awo": a[A + "Wout"].T,
        "w1": routed("w1"), "w3": routed("w3"), "shared": np.concatenate([a[F + "router_w"], shared("w1"), shared("w3")], axis=1),
        "w2": w2.reshape(CHUNKS, P, D).transpose(1, 0, 2).reshape(P, FF),
        "xbq": col(X + "wq_b"), "xbk": col(X + "wk_b"), "xbv": col(X + "wv_b"), "abq": col(A + "bq"), "abk": col(A + "bk"),
        "u": col(A + "u_bias"), "v": col(A + "v_bias"), "gamma": col(A + "ln_gamma"), "beta": col(A + "ln_beta"),
        **shape_tables(),
    }
    weights = np.ascontiguousarray(np.concatenate([parts[n] for n, _ in WEIGHT_BLOCKS], axis=1))
    vectors = {"xbv": a[X + "wv_b"], "xbo": a[X + "wo_b"], "ln_g": a[X + "ln_g"], "ln_b": a[X + "ln_b"],
               "abv": a[A + "bv"], "abo": a[A + "bout"], "rb": a[F + "router_b"]}
    rows = np.ascontiguousarray(np.concatenate([vectors[n] for n, _ in ROW_BLOCKS]))
    c = a["ctx_1024"]
    ctx_main = np.ascontiguousarray(c[:, :2 * P].reshape(TILES, BT, 2, P, D).transpose(0, 3, 1, 2, 4))
    ctx_last = np.ascontiguousarray(c[:, 2 * P])
    mask = np.ascontiguousarray(a["mask_Bx1xSxS2_bf0"]).reshape(NB, S * S2)
    arrays = {"in_x": np.ascontiguousarray(a["x"]), "in_ctx_main": ctx_main, "in_ctx_last": ctx_last,
              "in_mask": mask, "in_weights": weights, "in_rows": rows}

    nc = bacc.Bacc("TRN2", target_bir_lowering=False, num_devices=1)
    f32 = mybir.dt.float32
    args = [nc.dram_tensor(n, v.shape, mybir.dt.from_np(v.dtype), kind="ExternalInput").ap() for n, v in arrays.items()]
    out = nc.dram_tensor("out_x", (NB, S, D), f32, kind="ExternalOutput").ap()
    pos_scratch = nc.dram_tensor("pos_scratch", (NB, S, HEADS * S), f32, kind="Internal").ap()
    v_scratch = nc.dram_tensor("v_scratch", (S, TILES, BT, D), f32, kind="Internal").ap()
    piece_scratch = nc.dram_tensor("piece_scratch", (PIECES, NB, GW), mybir.dt.bfloat16, kind="Internal").ap()
    perceiver_kernel(nc, *args, out, pos_scratch, v_scratch, piece_scratch)
    r = run_bass_kernel_spmd(nc, [arrays], core_ids=[0])
    return r.results[0]["out_x"]
```
